# Optimizing a Trainium2 kernel written in Bass

```python
import numpy as np
import jax
import jax.numpy as jnp

def _softmax(x, axis=-1):
    return jax.nn.softmax(x, axis=axis)

def _gelu(x):
    return jax.nn.gelu(x, approximate=True)

def _silu(x):
    return jax.nn.silu(x)

def _sigmoid(x):
    return jax.nn.sigmoid(x)

def _layernorm(x, axis=-1, eps=1e-05):
    m = jnp.mean(x, axis=axis, keepdims=True)
    v = jnp.var(x, axis=axis, keepdims=True)
    return (x - m) / jnp.sqrt(v + eps)

def _scatter_add(tgt, idx, src, axis=0):
    return tgt.at[idx].add(src)

def _segment_sum(src, seg, n):
    return jax.ops.segment_sum(src, seg, n)
kernel_name = 'mk_gnn_resnorm_d2_gnn_r64_bb5e73'

def setup_inputs(seed: int=0):
    np.random.seed(seed)
    _w = jnp.asarray

    def _rec_inputs():
        import jax
        import jax.numpy as jnp
        _gk = jax.random.key(seed)
        x = -0.0003713 + 1 * jax.random.normal(jax.random.fold_in(_gk, 1), (50000, 256), jnp.float32)
        src = jax.random.randint(jax.random.fold_in(_gk, 2), (12500,), 0, 50000, jnp.int32)
        dst = jax.random.randint(jax.random.fold_in(_gk, 3), (12500,), 0, 50000, jnp.int32)
        _o = jnp.argsort(dst, stable=True)
        src = src[_o]
        dst = dst[_o]
        edge_attr_128 = -5.16925e-05 + 1.00005 * jax.random.normal(jax.random.fold_in(_gk, 12), (12500, 128), jnp.float32)
        edge_attr_256 = -8.16379e-05 + 0.999858 * jax.random.normal(jax.random.fold_in(_gk, 13), (12500, 256), jnp.float32)
        return (x, src, dst, edge_attr_128, edge_attr_256)
    x, src, dst, edge_attr_128, edge_attr_256 = _rec_inputs()

    def _L0_gnn_setup():
        import jax, jax.numpy as jnp
        import numpy as np
        N_SRC = 50000
        N_DST = 50000
        E = 6250
        D_IN = 256
        D_OUT = 256
        key = jax.random.key(seed)
        k1, k2, k3, k4, k5 = jax.random.split(key, 5)
        src_feats = jax.random.normal(k1, (N_SRC, D_IN), dtype=jnp.float32)
        edge_feats = jax.random.normal(k2, (E, D_IN), dtype=jnp.float32)
        src_idx = jax.random.randint(k3, (E,), 0, N_SRC, dtype=jnp.int32)
        dst_idx = jax.random.randint(k4, (E,), 0, N_DST, dtype=jnp.int32)
        fan_in, fan_out = (2 * D_IN, D_OUT)
        bound = np.sqrt(6.0 / (fan_in + fan_out))
        weights = jax.random.uniform(k5, (2 * D_IN, D_OUT), dtype=jnp.float32, minval=-bound, maxval=bound)
        h_bias = jnp.zeros((D_OUT,), dtype=jnp.float32)
        return {'src_feats': src_feats, 'edge_feats': edge_feats, 'src_idx': src_idx, 'dst_idx': dst_idx, 'weights': weights, 'h_bias': h_bias, 'num_dst': N_DST}
    _L0_gnn_all = _L0_gnn_setup()
    _L0_gnn_in = {k: v for k, v in _L0_gnn_all.items() if k in ('weights', 'h_bias')}
    del _L0_gnn_all

    def _L1_gnn_setup():
        import jax, jax.numpy as jnp
        import numpy as np
        N = 50000
        E = 12500
        DIN = 256
        DOUT = 256
        H = 4
        C = DOUT // H
        ED = 128
        EPS = 1e-16

        def _transformer_conv(x, src, dst, edge_attr, Wq, bq, Wk, bk, Wv, bv, We, be, Ws, bs):
            n = x.shape[0]
            q = (x @ Wq + bq).reshape(n, H, C)
            k = (x @ Wk + bk).reshape(n, H, C)
            v = (x @ Wv + bv).reshape(n, H, C)
            e = (edge_attr @ We + be).reshape(-1, H, C)
            k_j = k[src] + e
            q_i = q[dst]
            alpha = jnp.einsum('ehc,ehc->eh', q_i, k_j) / jnp.sqrt(jnp.asarray(C, dtype=x.dtype))
            amax = jax.ops.segment_max(alpha, dst, num_segments=n)
            amax = jnp.where(jnp.isfinite(amax), amax, 0.0)
            ex = jnp.exp(alpha - amax[dst])
            denom = jax.ops.segment_sum(ex, dst, num_segments=n)
            alpha = ex / (denom[dst] + EPS)
            msg = (v[src] + e) * alpha[..., None]
            out = jax.ops.segment_sum(msg, dst, num_segments=n)
            out = out.reshape(n, H * C)
            return out + x @ Ws + bs
        key = jax.random.key(seed)
        ks = jax.random.split(key, 32)
        w = lambda k, shp: jax.random.normal(k, shp, dtype=jnp.float32) * (1.0 / np.sqrt(shp[0]))
        b = lambda k, n_: jax.random.normal(k, (n_,), dtype=jnp.float32) * 0.01
        inp = {'x': jax.random.normal(ks[0], (N, DIN), dtype=jnp.float32), 'edge_index': jax.random.randint(ks[1], (2, E), 0, N, dtype=jnp.int32), 'edge_attr': jax.random.normal(ks[2], (E, ED), dtype=jnp.float32)}
        names = ['Wq', 'Wk', 'Wv', 'We', 'Ws']
        dims1 = [DIN, DIN, DIN, ED, DIN]
        dims2 = [DOUT, DOUT, DOUT, ED, DOUT]
        i = 3
        for nm, d in zip(names, dims1):
            inp[nm + '1'] = w(ks[i], (d, DOUT))
            i += 1
            inp['b' + nm[1:].lower() + '1'] = b(ks[i], DOUT)
            i += 1
        for nm, d in zip(names, dims2):
            inp[nm + '2'] = w(ks[i], (d, DOUT))
            i += 1
            inp['b' + nm[1:].lower() + '2'] = b(ks[i], DOUT)
            i += 1
        return inp
    _L1_gnn_all = _L1_gnn_setup()
    _L1_gnn_in = {k: v for k, v in _L1_gnn_all.items() if k in ('Wq1', 'bq1', 'Wk1', 'bk1', 'Wv1', 'bv1', 'We1', 'be1', 'Ws1', 'bs1', 'Wq2', 'bq2', 'Wk2', 'bk2', 'Wv2', 'bv2', 'We2', 'be2', 'Ws2', 'bs2')}
    del _L1_gnn_all
    return {'x': x, 'src': src, 'dst': dst, 'edge_attr_128': edge_attr_128, 'edge_attr_256': edge_attr_256, 'L0_gnn_weights': _L0_gnn_in['weights'], 'L0_gnn_h_bias': _L0_gnn_in['h_bias'], 'L1_gnn_Wq1': _L1_gnn_in['Wq1'], 'L1_gnn_bq1': _L1_gnn_in['bq1'], 'L1_gnn_Wk1': _L1_gnn_in['Wk1'], 'L1_gnn_bk1': _L1_gnn_in['bk1'], 'L1_gnn_Wv1': _L1_gnn_in['Wv1'], 'L1_gnn_bv1': _L1_gnn_in['bv1'], 'L1_gnn_We1': _L1_gnn_in['We1'], 'L1_gnn_be1': _L1_gnn_in['be1'], 'L1_gnn_Ws1': _L1_gnn_in['Ws1'], 'L1_gnn_bs1': _L1_gnn_in['bs1'], 'L1_gnn_Wq2': _L1_gnn_in['Wq2'], 'L1_gnn_bq2': _L1_gnn_in['bq2'], 'L1_gnn_Wk2': _L1_gnn_in['Wk2'], 'L1_gnn_bk2': _L1_gnn_in['bk2'], 'L1_gnn_Wv2': _L1_gnn_in['Wv2'], 'L1_gnn_bv2': _L1_gnn_in['bv2'], 'L1_gnn_We2': _L1_gnn_in['We2'], 'L1_gnn_be2': _L1_gnn_in['be2'], 'L1_gnn_Ws2': _L1_gnn_in['Ws2'], 'L1_gnn_bs2': _L1_gnn_in['bs2']}

def reference(x, src, dst, edge_attr_128, edge_attr_256, L0_gnn_weights, L0_gnn_h_bias, L1_gnn_Wq1, L1_gnn_bq1, L1_gnn_Wk1, L1_gnn_bk1, L1_gnn_Wv1, L1_gnn_bv1, L1_gnn_We1, L1_gnn_be1, L1_gnn_Ws1, L1_gnn_bs1, L1_gnn_Wq2, L1_gnn_bq2, L1_gnn_Wk2, L1_gnn_bk2, L1_gnn_Wv2, L1_gnn_bv2, L1_gnn_We2, L1_gnn_be2, L1_gnn_Ws2, L1_gnn_bs2):
    import jax
    import jax.numpy as jnp

    def _L0_gnn_ref(src_feats, edge_feats, src_idx, dst_idx, weights, h_bias, num_dst):
        import jax, jax.numpy as jnp
        import numpy as np
        N_SRC = 50000
        N_DST = 50000
        E = 6250
        D_IN = 256
        D_OUT = 256
        d = src_feats.shape[1]
        m = src_feats[src_idx] @ weights[:d] + edge_feats @ weights[d:]
        deg = jax.ops.segment_sum(jnp.ones((m.shape[0],), jnp.float32), dst_idx, num_segments=num_dst)
        norm = jnp.where(deg > 0, jax.lax.rsqrt(jnp.maximum(deg, 1.0)), 0.0)
        h = jax.ops.segment_sum(m * norm[dst_idx][:, None], dst_idx, num_segments=num_dst)
        return h + h_bias

    def _L1_gnn_ref(x, edge_index, edge_attr, Wq1, bq1, Wk1, bk1, Wv1, bv1, We1, be1, Ws1, bs1, Wq2, bq2, Wk2, bk2, Wv2, bv2, We2, be2, Ws2, bs2):
        import jax, jax.numpy as jnp
        import numpy as np
        N = 50000
        E = 12500
        DIN = 256
        DOUT = 256
        H = 4
        C = DOUT // H
        ED = 128
        EPS = 1e-16

        def _transformer_conv(x, src, dst, edge_attr, Wq, bq, Wk, bk, Wv, bv, We, be, Ws, bs):
            n = x.shape[0]
            q = (x @ Wq + bq).reshape(n, H, C)
            k = (x @ Wk + bk).reshape(n, H, C)
            v = (x @ Wv + bv).reshape(n, H, C)
            e = (edge_attr @ We + be).reshape(-1, H, C)
            k_j = k[src] + e
            q_i = q[dst]
            alpha = jnp.einsum('ehc,ehc->eh', q_i, k_j) / jnp.sqrt(jnp.asarray(C, dtype=x.dtype))
            amax = jax.ops.segment_max(alpha, dst, num_segments=n)
            amax = jnp.where(jnp.isfinite(amax), amax, 0.0)
            ex = jnp.exp(alpha - amax[dst])
            denom = jax.ops.segment_sum(ex, dst, num_segments=n)
            alpha = ex / (denom[dst] + EPS)
            msg = (v[src] + e) * alpha[..., None]
            out = jax.ops.segment_sum(msg, dst, num_segments=n)
            out = out.reshape(n, H * C)
            return out + x @ Ws + bs
        src, dst = (edge_index[0], edge_index[1])
        h = _transformer_conv(x, src, dst, edge_attr, Wq1, bq1, Wk1, bk1, Wv1, bv1, We1, be1, Ws1, bs1)
        h = jax.nn.relu(h)
        out = _transformer_conv(h, src, dst, edge_attr, Wq2, bq2, Wk2, bk2, Wv2, bv2, We2, be2, Ws2, bs2)
        return out
    edge_index = jnp.stack([src, dst])
    x = _layernorm(x + _L0_gnn_ref(x, edge_attr_256, src, dst, L0_gnn_weights, L0_gnn_h_bias, 50000), axis=-1)
    x = _layernorm(x + _L1_gnn_ref(x, edge_index, edge_attr_128, L1_gnn_Wq1, L1_gnn_bq1, L1_gnn_Wk1, L1_gnn_bk1, L1_gnn_Wv1, L1_gnn_bv1, L1_gnn_We1, L1_gnn_be1, L1_gnn_Ws1, L1_gnn_bs1, L1_gnn_Wq2, L1_gnn_bq2, L1_gnn_Wk2, L1_gnn_bk2, L1_gnn_Wv2, L1_gnn_bv2, L1_gnn_We2, L1_gnn_be2, L1_gnn_Ws2, L1_gnn_bs2), axis=-1)
    return x

_drawn_inputs = setup_inputs


def setup_inputs(seed=0):
    import zlib

    import numpy as np

    out = dict(_drawn_inputs(seed))
    spreads = {'L0_gnn_h_bias': (0.0, 0.1)}
    factors = {'L1_gnn_bq1': 64.0,
     'L1_gnn_bk1': 64.0,
     'L1_gnn_bv1': 32.649,
     'L1_gnn_be1': 30.41,
     'L1_gnn_bs1': 8.0,
     'L1_gnn_bq2': 64.0,
     'L1_gnn_bk2': 64.0,
     'L1_gnn_bv2': 24.462,
     'L1_gnn_be2': 24.736,
     'L1_gnn_bs2': 8.0}
    for name, (base, spread) in spreads.items():
        noise = np.random.default_rng([zlib.crc32(name.encode()), seed]).standard_normal(out[name].shape)
        drawn = base * np.exp(spread * noise) if base else spread * noise
        out[name] = jnp.asarray(drawn.astype(out[name].dtype))
    for name, factor in factors.items():
        out[name] = (out[name] * factor).astype(out[name].dtype)
    return out
```

```python
import numpy as np
import concourse.bass as bass
import concourse.mybir as mybir
from contextlib import ExitStack

F32 = mybir.dt.float32
BF16 = mybir.dt.bfloat16
I32 = mybir.dt.int32
ALU = mybir.AluOpType
ACT = mybir.ActivationFunctionType
AX = mybir.AxisListType

P = 128
N, D, ED, H, E = 50000, 256, 128, 4, 12500
C = D // H
EPT = P - 1
EB = 4
TILES = EB * -(-E // (EB * EPT))
J = 4
GROUP = P * J
GROUPS = -(-N // GROUP)
DB = 4
LN_EPS = 1e-5
SOFTMAX_EPS = 1e-16
BIG = float(2 ** 100)
CW = D + H


def build(nc, a, out):
    ctx = ExitStack()
    with ctx:
        def sb(name, shape, dt=F32):
            return ctx.enter_context(nc.sbuf_tensor(name, shape, dt))

        def pb(name):
            return ctx.enter_context(nc.psum_tensor(name, [P, 512], F32))

        def sem(name):
            return ctx.enter_context(nc.semaphore(name))

        def sems(name, n):
            return [sem(f"{name}{i}") for i in range(n)]

        x1_table = nc.dram_tensor("x1_table", [N, D], F32).ap()
        h_table = nc.dram_tensor("h_table", [N, D], F32).ap()
        x1_spill = nc.dram_tensor("x1_spill", [TILES, P, D], F32).ap()
        self_spill = [nc.dram_tensor(f"self_spill{l}", [TILES, P, D], F32).ap() for l in range(2)]

        ident = sb("ident", [P, P])
        ones_bf = sb("ones_bf", [P, P], BF16)
        w0 = sb("w0", [P, 4, D])
        w_qs = [sb(f"w_qs{l}", [P, 2, 2 * D]) for l in range(2)]
        w_kv = [sb(f"w_kv{l}", [P, 2, 2 * D]) for l in range(2)]
        w_e = [sb(f"w_e{l}", [P, D]) for l in range(2)]
        b0_all = sb("b0_all", [P, D])
        bias_mm = sb("bias_mm", [P, 4, 2 * D], BF16)
        src_idx = sb("src_idx", [P, TILES], I32)
        dst_idx = sb("dst_idx", [P, TILES], I32)
        dst_next = sb("dst_next", [P, TILES], I32)
        dst_f = sb("dst_f", [P, TILES])
        last_idx = sb("last_idx", [P, TILES], I32)
        alpha = sb("alpha", [P, TILES * H])
        ex = sb("ex", [P, TILES * H])

        GD = J * D
        vals = sb("vals", [P, TILES * D])
        assert 6 * DB * GD <= TILES * D

        def dense_buf(i):
            return vals[:, i * DB * GD:(i + 1) * DB * GD].rearrange("p (b n) -> p b n", b=DB)
        d_x, d_x1, d_x1T, d_h, d_hT, d_y = (dense_buf(i) for i in range(6))

        bias_row = d_h[0:1, :, :].rearrange("o b n -> o (b n)")[:, 0:12 * D].rearrange("o (r n) -> o r n", r=6)
        bias_hi = d_y[0:1, :, :].rearrange("o b n -> o (b n)")[:, 0:12 * D].bitcast(BF16).rearrange(
            "o (i r n) -> o i r n", i=4, r=3)

        d_st = sb("d_st", [P, 2, J, 6])
        d_mv = sb("d_mv", [P, 2, J, 2])
        d_dev = sb("d_dev", [P, 2, J])
        d_rs = sb("d_rs", [P, 2, 2, J])

        e_src = sb("e_src", [P, EB, D])
        e_dst = sb("e_dst", [P, EB, D])
        e_res = sb("e_res", [P, EB, D])
        e_attr = sb("e_attr", [P, EB, D])
        e_inT = sb("e_inT", [P, EB, 4 * P])
        e_atT = sb("e_atT", [P, EB, P])
        zero_row = sb("zero_row", [1, CW])
        ln_eps = sb("ln_eps", [P, 1])
        e_rhs = sb("e_rhs", [P, EB, CW])
        e_rhs0 = sb("e_rhs0", [P, EB, D + 1])
        e_row = sb("e_row", [P, EB, P], I32)
        e_eq = sb("e_eq", [P, EB, P])
        e_qs = sb("e_qs", [P, EB, 2 * D])
        e_prod = sb("e_prod", [P, D])
        e_z = sb("e_z", [P, EB, D])
        e_o = sb("e_o", [P, EB, D])
        e_st = sb("e_st", [P, 6])
        e_mv = sb("e_mv", [P, EB, 2])
        e_sd = sb("e_sd", [P, EB])
        e_dev = sb("e_dev", [P, EB])
        e_rs = sb("e_rs", [P, EB, 2])
        e_nrm = sb("e_nrm", [P, 4])
        e_sx = [sb(f"e_sx{i}", [P, 1], I32) for i in range(EB)]
        e_rx = [sb(f"e_rx{i}", [P, 1], I32) for i in range(EB)]
        e_dx = [sb(f"e_dx{i}", [P, 1], I32) for i in range(EB)]
        e_lx = [sb(f"e_lx{i}", [P, 1], I32) for i in range(EB)]

        m_dst = sb("m_dst", [TILES, P + 2], I32)
        m_same = sb("m_same", [TILES, 2, P])
        m_a = sb("m_a", [TILES, H * P])
        m_f = sb("m_f", [TILES, H * P])
        m_r = sb("m_r", [TILES, H * P])
        m_end = sb("m_end", [TILES, P])
        m_edge = sb("m_edge", [64, 4, TILES], I32)
        m_gate = sb("m_gate", [64, 2, TILES])
        m_rows = sb("m_rows", [64, TILES])
        m_scan = sb("m_scan", [64, TILES])
        m_in = sb("m_in", [64, TILES])
        m_cin = sb("m_cin", [TILES, 64])

        bank = [pb(f"bank{i}") for i in range(8)]
        T_BANK, W_BANK = (0, 1), (2, 3)
        GT_BANK, GM_BANK, GTOT_BANK = 4, 5, (6, 7)

        weights_in = sem("weights_in")
        biases_in = sem("biases_in")
        b0_in = sem("b0_in")
        index_in = sem("index_in")
        ends_in = sem("ends_in")
        ident_done = sem("ident_done")
        pads_done = sem("pads_done")
        prep_done = sem("prep_done")
        split_step = sem("split_step")
        bias_moved = sem("bias_moved")

        x_loaded = sems("x_loaded", DB)
        x1_stored = sems("x1_stored", DB)
        h_stored = sems("h_stored", DB)
        y_stored = sems("y_stored", DB)
        x_biased = sem("x_biased")
        x_step = sem("x_step")
        y_step = sem("y_step")
        dev_done = sems("dev_done", 2)
        factor_step = sems("factor_step", 2)
        x1_done = sem("x1_done")
        x1T_psum = sem("x1T_psum")
        x1T_act = sem("x1T_act")
        x1T_dve = sem("x1T_dve")
        h_psum = sem("h_psum")
        h_done = sem("h_done")
        hT_psum = sem("hT_psum")
        hT_act = sem("hT_act")
        hT_dve = sem("hT_dve")
        y_psum = sem("y_psum")
        y_done = sem("y_done")

        slot = {n: sems(n, EB) for n in ("src_in", "dst_in", "attr_in", "row_in", "res_in", "self_in", "spilled", "scattered")}
        USES = TILES // EB

        def edge_sems(ph, counts, **before):
            d = {n: sem(f"{ph}_{n}") for n in counts}
            d["before"] = before
            return d
        G0 = edge_sems("g", ("src_in_ix", "dst_in_ix", "T_psum", "T_out", "M_psum", "rhs_in", "carry", "eq", "tot", "deg",
                             "fin", "dev", "factor", "o"), src_in=0, dst_in=0, attr_in=0, row_in=0, spilled=0)
        R0 = edge_sems("r", ("lx",), self_in=0, scattered=0)
        A = [edge_sems(f"a{l}", ("src_in_ix", "dst_in_ix", "T_psum", "T_out", "aT_out", "qs_psum", "k_psum", "v_psum",
                                 "qs_out", "v_out", "score") + (("res_in_ix", "res_added") if l else ()),
                       src_in=1 + l, dst_in=1 + l, attr_in=1 + l, res_in=0, spilled=1 + l) for l in range(2)]
        CB = [edge_sems(f"c{l}", ("lx", "weighed", "carry", "eq", "tot", "fin", "o") + (("dev", "factor") if l else ()),
                        row_in=1 + l, self_in=1 + l, scattered=1 + l) for l in range(2)]
        SM = [edge_sems(f"s{l}", ("masked", "aT", "step", "ends", "cin", "max_psum", "max", "exp")) for l in range(2)]
        settled = sem("settled")
        m_step = sem("m_step")
        idx_step = sem("idx_step")

        def at(i, o, n):
            return n * i + o, i + o // n, o % n

        def settle(eng):
            eng.sem_inc(settled)

        def skip(i, o, total):
            return isinstance(i, int) and not 0 <= o < total

        def freed(eng, s, i, o, n, times=1):
            if isinstance(i, int) and o < n:
                return
            eng.wait_ge(s, (UNROLL * i + o - n + 1) * times)

        def arrived(eng, s, what, k, b):
            eng.wait_ge(slot[what][b], 16 * (k + s["before"][what] * USES + 1))

        def over(eng, s, what, k, b):
            eng.wait_ge(slot[what][b], 16 * (k + s["before"][what] * USES))

        def all_over(eng, s, what):
            for b in range(EB):
                eng.wait_ge(slot[what][b], 16 * USES * (s["before"][what] + 1))

        def run(eng, f, total, back, ahead, more=0):
            start = back + UNROLL
            rounds = (total - ahead - start) // UNROLL
            for o in range(-ahead, start):
                f(0, o)
            with eng.Fori(0, rounds) as i:
                for o in range(start, start + UNROLL):
                    f(i, o)
            for o in range(start + rounds * UNROLL, total + more + back):
                f(0, o)

        class Chain:
            def __init__(self, eng, s, item, steps):
                self.eng, self.s, self.base, self.steps, self.j = eng, s, item * steps, steps, 0

            def add(self, ins):
                self.j += 1
                ins.then_inc(self.s, 1)
                if self.j < self.steps:
                    self.eng.wait_ge(self.s, self.base + self.j)

        X_STEPS, Y_STEPS = 2, 4
        FIN_STEPS = (6, 4, 6)

        def dense_base(i, o):
            return N - GROUP if isinstance(i, int) and o == GROUPS - 1 else GROUP * (DB * i + o)

        def node_rows(t, base, lo=0):
            return t[bass.ds(base + lo * J, (P - lo) * J), :].rearrange("(p j) d -> p (j d)", j=J)

        def tile_of(t, n):
            return t[bass.ds(n, 1), :, :].rearrange("o p d -> (o p) d")

        def all_uses(b, total):
            return 16 * len(range(b, total, DB))

        block = ctx.enter_context(nc.Block())

        @block.sync
        def _(sp):
            sp.dma_start(b0_all[:, :], a["L0_gnn_h_bias"].rearrange("(o n) -> o n", o=1).to_broadcast([P, D])).then_inc(b0_in, 16)

            def load_x(i, o):
                if skip(i, o, GROUPS):
                    return
                g, k, b = at(i, o, DB)
                freed(sp, x1_done, i, o, DB)
                sp.dma_start(d_x[:, b, :], node_rows(a["x"], dense_base(i, o))).then_inc(x_loaded[b], 16)
            for o in range(2):
                load_x(0, o)
            for l in range(2):
                s = str(l + 1)
                for w, t, o in (("Ws", w_qs, D), ("Wq", w_qs, 0), ("Wk", w_kv, 0), ("Wv", w_kv, D)):
                    sp.dma_start(t[l][:, :, o:o + D],
                                 a["L1_gnn_" + w + s].rearrange("(k p) n -> p k n", p=P)).then_inc(weights_in, 16)
                sp.dma_start(w_e[l][:, :], a["L1_gnn_We" + s]).then_inc(weights_in, 16)
                for r, b, o in ((0, "bq", 0), (0, "bs", D), (1, "bk", 0), (1, "bv", D), (2, "be", 0), (2, "be", D)):
                    sp.dma_start(bias_row[0:1, 3 * l + r, o:o + D],
                                 a["L1_gnn_" + b + s].rearrange("(o n) -> o n", o=1)).then_inc(biases_in, 16)
            sp.dma_start(w0[:, :, :], a["L0_gnn_weights"].rearrange("(k p) n -> p k n", p=P)).then_inc(weights_in, 16)
            for t, s in ((src_idx, "src_slots"), (dst_idx, "dst_slots"), (dst_next, "dst_next")):
                sp.dma_start(t[:, :], a[s]).then_inc(index_in, 16)
            sp.dma_start(m_dst[:, :], a["dst_tiles"]).then_inc(ends_in, 16)
            for r in range(4):
                sp.dma_start(m_edge[:, r, :], a["tile_ends"][r:r + 1, :].to_broadcast([64, TILES])).then_inc(ends_in, 16)
            sp.wait_ge(split_step, SPLIT_STEPS)
            sp.wait_ge(prep_done, 1)
            for i in range(4):
                sp.dma_start(bias_mm[0:3, i, :], bias_hi[0:1, i, :, :]).then_inc(bias_moved, 16)

            def store(i, o, src, table, done, stored):
                if skip(i, o, GROUPS):
                    return
                g, k, b = at(i, o, DB)
                sp.wait_ge(done, g + 1)
                lo = (GROUPS * GROUP - N) // J if isinstance(i, int) and o == GROUPS - 1 else 0
                sp.dma_start(node_rows(table, dense_base(i, o), lo), src[lo:, b, :]).then_inc(stored[b], 16)

            def load_row(s, i, o):
                if skip(i, o, TILES):
                    return
                t, k, b = at(i, o, EB)
                freed(sp, s["eq"], i, o, EB)
                settle(sp)
                sp.dma_start(e_row[:, b, :], a["dst_rows"][bass.ds(t, 1), :].to_broadcast([P, P])).then_inc(slot["row_in"][b], 16)

            def load_attr(s, attr, width, i, o):
                if skip(i, o, TILES):
                    return
                t, k, b = at(i, o, EB)
                freed(sp, s["T_psum"], i, o, EB)
                sp.dma_start(e_attr[:, b, 0:width], attr[bass.ds(t * P, P), :]).then_inc(slot["attr_in"][b], 16)

            def spill(s, done, src, table, i, o):
                if skip(i, o, TILES):
                    return
                t, k, b = at(i, o, EB)
                sp.wait_ge(done, t + 1)
                sp.dma_start(tile_of(table, t), src(b)).then_inc(slot["spilled"][b], 16)

            def first_pass(i, o):
                load_attr(G0, a["attr_256"], 2 * ED, i, o + 3)
                load_row(G0, i, o + 2)
                if not (isinstance(i, int) and o + 5 < 2):
                    load_x(i, o + 5)
                store(i, o, d_h, h_table, h_done, h_stored)
                store(i, o - 2, d_y, out, y_done, y_stored)
                store(i, o + 2, d_x1, x1_table, x1_done, x1_stored)
                spill(G0, G0["o"], lambda b: e_o[:, b, :], x1_spill, i, o - 3)
            run(sp, first_pass, GROUPS, 3, 5, TILES - GROUPS)

            all_over(sp, G0, "spilled")

            def reload(i, o):
                t, k, b = at(i, o, EB)
                if not (isinstance(i, int) and o < EB):
                    over(sp, R0, "scattered", k, b)
                sp.dma_start(e_res[:, b, :], tile_of(x1_spill, t)).then_inc(slot["self_in"][b], 16)
            run(sp, reload, TILES, 0, 0)

            sp.wait_ge(G0["T_psum"], TILES)
            for l in range(2):
                def attend(i, o):
                    load_attr(A[l], a["attr_128"], ED, i, o + 3)
                    spill(A[l], A[l]["res_added" if l else "qs_out"], lambda b: e_qs[:, b, D:2 * D], self_spill[l], i, o)
                run(sp, attend, TILES, 0, 3)
                all_over(sp, A[l], "spilled")

                def combine(i, o):
                    t, k, b = at(i, o, EB)
                    load_row(CB[l], i, o)
                    freed(sp, CB[l]["fin"], i, o, EB, FIN_STEPS[1 + l])
                    sp.dma_start(e_res[:, b, :], tile_of(self_spill[l], t)).then_inc(slot["self_in"][b], 16)
                if l == 0:
                    all_over(sp, R0, "scattered")
                run(sp, combine, TILES, 0, 0)

        @block.gpsimd
        def _(pool):
            nc.gpsimd.memset(ident[:, :], 0.0).then_inc(ident_done, 1)
            pool.wait_ge(ident_done, 1)
            nc.gpsimd.affine_select(out=ident[:, :], in_=ident[:, :], compare_op=ALU.not_equal, fill=1.0,
                                    base=0, pattern=[[-1, P]], channel_multiplier=1).then_inc(ident_done, 1)
            for t in (e_src, e_dst, e_res):
                nc.gpsimd.memset(t[:, :, :], 0.0).then_inc(pads_done, 1)
            pool.wait_ge(b0_in, 16)

            def bias(i, o):
                if skip(i, o, GROUPS):
                    return
                g, k, b = at(i, o, DB)
                pool.wait_ge(x_loaded[b], 16 * k + 16)
                v = d_x[:, b, :].rearrange("p (j d) -> p j d", j=J)
                nc.gpsimd.tensor_tensor(v, v, b0_all[:, None, :].to_broadcast([P, J, D]), ALU.add).then_inc(x_biased, 1)

            def gather(s, what, buf, table, index, ix, free, i, o):
                if skip(i, o, TILES):
                    return
                t, k, b = at(i, o, EB)
                freed(pool, free[0], i, o, EB, free[1])
                over(pool, s, what, k, b)
                settle(pool)
                nc.gpsimd.tensor_copy(ix[b][:, :], index[:, bass.ds(t, 1)]).then_inc(s[what + "_ix"], 1)
                pool.wait_ge(s[what + "_ix"], t + 1)
                settle(pool)
                nc.gpsimd.indirect_dma_start(out=buf[:, b, :], out_offset=None, in_=table,
                                             in_offset=bass.IndirectOffsetOnAxis(ap=ix[b][:, :], axis=0),
                                             bounds_check=N - 1, oob_is_err=False).then_inc(slot[what][b], 16)

            def scatter(s, table, rows, ready, i, o):
                if skip(i, o, TILES):
                    return
                t, k, b = at(i, o, EB)
                over(pool, s, "scattered", k, b)
                settle(pool)
                nc.gpsimd.tensor_copy(e_lx[b][:, :], last_idx[:, bass.ds(t, 1)]).then_inc(s["lx"], 1)
                pool.wait_ge(s["lx"], t + 1)
                ready(t, k, b)
                settle(pool)
                nc.gpsimd.indirect_dma_start(out=table, out_offset=bass.IndirectOffsetOnAxis(ap=e_lx[b][:, :], axis=0),
                                             in_=rows[:, b, :], in_offset=None,
                                             bounds_check=N - 1, oob_is_err=False).then_inc(slot["scattered"][b], 16)

            def first_pass(i, o):
                if isinstance(i, int) and o == -3:
                    pool.wait_ge(pads_done, 3)
                    pool.wait_ge(index_in, 48)
                    pool.wait_ge(idx_step, 3)
                gather(G0, "src_in", e_src, a["x"], src_idx, e_sx, (G0["T_psum"], 1), i, o + 3)
                gather(G0, "dst_in", e_dst, a["x"], dst_idx, e_dx, (G0["fin"], FIN_STEPS[0]), i, o + 2)
                bias(i, o + 4)
            run(pool, first_pass, GROUPS, 0, 4, TILES - GROUPS)

            for b in range(DB):
                for stored in (x1_stored, h_stored, y_stored):
                    pool.wait_ge(stored[b], all_uses(b, GROUPS))
            run(pool, lambda i, o: scatter(R0, x1_table, e_res, lambda t, k, b: arrived(pool, R0, "self_in", k, b), i, o),
                TILES, 0, 0)
            all_over(pool, R0, "scattered")
            for l in range(2):
                table, residual = ((x1_table, None), (h_table, x1_table))[l]

                def attend(i, o):
                    gather(A[l], "src_in", e_src, table, src_idx, e_sx, (A[l]["T_psum"], 1), i, o)
                    gather(A[l], "dst_in", e_dst, table, dst_idx, e_dx, (A[l]["T_psum"], 1), i, o)
                    if residual is not None:
                        gather(A[l], "res_in", e_res, residual, dst_idx, e_rx, (A[l]["res_added"], 1), i, o - 2)
                run(pool, attend, TILES, 2 * l, 0)
                pool.wait_ge(SM[l]["exp"], 1)

                def weigh(i, o):
                    if skip(i, o, TILES):
                        return
                    t, k, b = at(i, o, EB)
                    freed(pool, CB[l]["tot"], i, o, EB)
                    w = ex[:, bass.ds(t * H, H)]
                    settle(pool)
                    nc.gpsimd.tensor_copy(e_rhs[:, b, D:CW], w)
                    nc.gpsimd.tensor_tensor(e_rhs[:, b, 0:D].rearrange("p (h c) -> p h c", h=H),
                                            vals[:, bass.ds(t * D, D)].rearrange("p (h c) -> p h c", h=H),
                                            w.rearrange("p (h o) -> p h o", o=1).to_broadcast([P, H, C]),
                                            ALU.mult).then_inc(CB[l]["weighed"], 1)

                def combine(i, o):
                    weigh(i, o + 3)
                    scatter(CB[l], out if l else h_table, e_o, lambda t, k, b: pool.wait_ge(CB[l]["o"], t + 1), i, o - 2 - l)
                run(pool, combine, TILES, 2 + l, 3)
                all_over(pool, CB[l], "scattered")

        @block.scalar
        def _(act):
            def norm_rows(which, i, o):
                if skip(i, o, GROUPS):
                    return
                g, k, b = at(i, o, DB)
                act.wait_ge(factor_step[which], 2 * g + 2)
                if which == 0:
                    act.wait_ge(x1_stored[b], 16 * k)
                    freed(act, y_step, i, o, DB, Y_STEPS)
                src, dst = (d_x, d_x1) if which == 0 else (d_y, d_y)
                for j in range(J):
                    last = nc.scalar.activation(dst[:, b, j * D:(j + 1) * D], src[:, b, j * D:(j + 1) * D], ACT.Identity,
                                                bias=d_rs[:, which, 1, j:j + 1], scale=d_rs[:, which, 0, j:j + 1])
                last.then_inc((x1_done, y_done)[which], 1)

            def deviations(which, i, o):
                if skip(i, o, GROUPS):
                    return
                g = at(i, o, DB)[0]
                steps = (X_STEPS, Y_STEPS)[which]
                act.wait_ge((x_step, y_step)[which], steps * (g + 1))
                if not (isinstance(i, int) and o < 1):
                    act.wait_ge(factor_step[which], 2 * g)
                nc.scalar.activation(d_dev[:, which, :], d_mv[:, which, :, 1], ACT.Sqrt, bias=ln_eps[:, 0:1]).then_inc(dev_done[which], 1)

            def relu_h(i, o):
                if skip(i, o, GROUPS):
                    return
                g, k, b = at(i, o, DB)
                act.wait_ge(h_stored[b], 16 * k)
                for m in range(2):
                    act.wait_ge(h_psum, 2 * g + m + 1)
                    last = nc.scalar.activation(d_h[:, b, m * 2 * D:(m + 1) * 2 * D], bank[W_BANK[m]][:, :], ACT.Relu)
                last.then_inc(h_done, 1)

            def half(psum, done, used, dst, i, o):
                if skip(i, o, GROUPS):
                    return
                g, k, b = at(i, o, DB)
                act.wait_ge(psum, g + 1)
                freed(act, used, i, o, DB, 2)
                nc.scalar.activation(dst[:, b, 0:GROUP], bank[T_BANK[0]][:, :], ACT.Copy).then_inc(done, 1)

            def inT_out(s, used, src, i, o):
                if skip(i, o, TILES):
                    return
                t, k, b = at(i, o, EB)
                act.wait_ge(s["T_psum"], t + 1)
                freed(act, s[used], i, o, EB)
                nc.scalar.activation(e_inT[:, b, :], src[:, :], ACT.Copy).then_inc(s["T_out"], 1)

            def carry(s, below, rhs, width, tot, i, o):
                t, k, b = at(i, o, EB)
                act.wait_ge(below, t + 1)
                if isinstance(i, int) and o == 0:
                    src = zero_row[0:1, 0:width]
                else:
                    act.wait_ge(s["tot"], t)
                    src = tot[0:1, 0:width]
                nc.scalar.activation(rhs[0:1, b, 0:width], src, ACT.Copy).then_inc(s["carry"], 1)

            def deviation(s, steps, i, o):
                if skip(i, o, TILES):
                    return
                t, k, b = at(i, o, EB)
                act.wait_ge(s["fin"], steps * (t + 1))
                freed(act, s["factor"], i, o, EB, 2)
                nc.scalar.activation(e_dev[:, b:b + 1], e_mv[:, b, 1:2], ACT.Sqrt, bias=ln_eps[:, 0:1]).then_inc(s["dev"], 1)

            def finish(s, what, relu, i, o):
                if skip(i, o, TILES):
                    return
                t, k, b = at(i, o, EB)
                if relu:
                    act.wait_ge(s["fin"], FIN_STEPS[1] * (t + 1))
                else:
                    act.wait_ge(s["factor"], 2 * (t + 1))
                over(act, s, what, k, b)
                if relu:
                    nc.scalar.activation(e_o[:, b, :], e_z[:, b, :], ACT.Relu).then_inc(s["o"], 1)
                else:
                    nc.scalar.activation(e_o[:, b, :], e_z[:, b, :], ACT.Identity,
                                         bias=e_rs[:, b, 1:2], scale=e_rs[:, b, 0:1]).then_inc(s["o"], 1)

            def g_operand(i, o):
                if skip(i, o, TILES):
                    return
                t, k, b = at(i, o, EB)
                act.wait_ge(G0["M_psum"], t + 1)
                freed(act, G0["tot"], i, o, EB)
                nc.scalar.activation(e_rhs0[:, b, 0:D], bank[GM_BANK][:, 0:D], ACT.Copy).then_inc(G0["rhs_in"], 1)
                carry(G0, G0["rhs_in"], e_rhs0, D + 1, bank[GTOT_BANK[(b + 1) % 2]], i, o)

            def g_degree(i, o):
                if skip(i, o, TILES):
                    return
                t, k, b = at(i, o, EB)
                act.wait_ge(G0["tot"], t + 1)
                freed(act, G0["fin"], i, o, EB, FIN_STEPS[0])
                nc.scalar.activation(e_sd[:, b:b + 1], bank[GTOT_BANK[b % 2]][:, D:D + 1], ACT.Sqrt).then_inc(G0["deg"], 1)

            def first_pass(i, o):
                g_operand(i, o - 1)
                g_degree(i, o - 2)
                deviations(1, i, o - 2)
                relu_h(i, o)
                deviations(0, i, o + 2)
                half(x1T_psum, x1T_act, h_psum, d_x1T, i, o + 1)
                inT_out(G0, "M_psum", bank[GT_BANK], i, o + 1)
                norm_rows(1, i, o - 2)
                norm_rows(0, i, o + 2)
                deviation(G0, FIN_STEPS[0], i, o - 2)
                finish(G0, "spilled", False, i, o - 3)
                half(hT_psum, hT_act, y_psum, d_hT, i, o)
            act.wait_ge(prep_done, 5)
            run(act, first_pass, GROUPS, 3, 2, TILES - GROUPS)

            for l in range(2):
                s, c = A[l], CB[l]

                def attend(i, o):
                    inT_out(s, "v_psum", bank[(o + 1) % 2], i, o + 1)
                    if skip(i, o, TILES):
                        return
                    t, k, b = at(i, o, EB)
                    act.wait_ge(s["qs_psum"], t + 1)
                    freed(act, s["score"], i, o, EB, 2)
                    over(act, s, "spilled", k, b)
                    nc.scalar.activation(e_qs[:, b, :], bank[5 + b % 2][:, :], ACT.Copy).then_inc(s["qs_out"], 1)
                    act.wait_ge(s["v_psum"], t + 1)
                    settle(act)
                    nc.scalar.activation(vals[:, bass.ds(t * D, D)], bank[(2, 7)[b % 2]][:, 0:D], ACT.Copy).then_inc(s["v_out"], 1)
                run(act, attend, TILES, 0, 1)

                act.wait_ge(SM[l]["max"], 1)
                nc.scalar.activation(ex[:, :], ex[:, :], ACT.Exp, scale=float(C) ** -0.5).then_inc(SM[l]["exp"], 1)

                def combine(i, o):
                    if not skip(i, o, TILES):
                        carry(c, c["weighed"], e_rhs, CW, bank[(o - 1) % EB], i, o)
                    if l:
                        deviation(c, FIN_STEPS[2], i, o - 2)
                    finish(c, "scattered", l == 0, i, o - 2 - l)
                run(act, combine, TILES, 2 + l, 0)

        @block.vector
        def _(dve):
            nc.vector.memset(bias_mm[:, :, :], 0.0).then_inc(prep_done, 1)
            nc.vector.memset(zero_row[:, :], 0.0).then_inc(prep_done, 1)
            nc.vector.memset(ln_eps[:, :], LN_EPS).then_inc(prep_done, 1)
            nc.vector.memset(e_rhs0[:, :, :], 1.0).then_inc(prep_done, 1)
            nc.vector.memset(ones_bf[:, :], 1.0).then_inc(prep_done, 1)

            ch = Chain(dve, split_step, 0, SPLIT_STEPS)
            dve.wait_ge(biases_in, 16 * 12)
            for l in range(2):
                r = bias_row[0:1, 3 * l:3 * l + 3, :]
                ch.add(nc.vector.tensor_tensor(r[:, 1, :], r[:, 1, :], r[:, 2, :], ALU.add))
                for m in range(2):
                    for part in range(3):
                        ch.add(nc.vector.tensor_copy(bias_hi[0:1, 2 * l + m, part, :], r[:, m, :]))
                        if part < 2:
                            ch.add(nc.vector.tensor_tensor(r[:, m, :], r[:, m, :], bias_hi[0:1, 2 * l + m, part, :], ALU.subtract))

            dve.wait_ge(index_in, 48)
            ch = Chain(dve, idx_step, 0, 3)
            ch.add(nc.vector.tensor_copy(dst_f[:, :], dst_idx[:, :]))
            ch.add(nc.vector.tensor_tensor(last_idx[:, :], dst_next[:, :], dst_idx[:, :], ALU.is_equal))
            ch.add(nc.vector.scalar_tensor_tensor(last_idx[:, :], last_idx[:, :], float(N), dst_idx[:, :], ALU.mult, ALU.add))

            dve.wait_ge(ends_in, 16 * 5)
            ch = Chain(dve, m_step, 0, 13)
            for r, lo in ((0, 0), (1, 2)):
                ch.add(nc.vector.tensor_tensor(m_same[:, r, :], m_dst[:, 1:P + 1], m_dst[:, lo:lo + P], ALU.is_equal))
                ch.add(nc.vector.tensor_scalar(m_same[:, r, :], m_same[:, r, :], 2 * BIG, -BIG, ALU.mult, ALU.add))
            first, last, prev_last, next_first = (m_edge[:, r, :] for r in range(4))
            for g, x, y in ((0, last, prev_last), (1, first, prev_last)):
                ch.add(nc.vector.tensor_tensor(m_gate[0:32, g, :], x[0:32], y[0:32], ALU.is_equal))
                ch.add(nc.vector.tensor_scalar(m_gate[0:32, g, :], m_gate[0:32, g, :], 2 * BIG, -BIG, ALU.mult, ALU.add))
            for g, x, y in ((0, first, next_first), (1, last, next_first)):
                ch.add(nc.vector.tensor_tensor(m_gate[32:64, g, :], x[32:64], y[32:64], ALU.is_equal))
                ch.add(nc.vector.tensor_scalar(m_gate[32:64, g, :], m_gate[32:64, g, :], 2 * BIG, -BIG, ALU.mult, ALU.add))
            ch.add(nc.vector.memset(m_end[:, :], 0.0))

            def factors(ch, rs_scale, rs_bias, mean, deviation):
                ch.add(nc.vector.reciprocal(rs_scale, deviation))
                ch.add(nc.vector.scalar_tensor_tensor(rs_bias, mean, -1.0, rs_scale, ALU.mult, ALU.mult))

            def group_factors(which, i, o):
                if skip(i, o, GROUPS):
                    return
                g = at(i, o, DB)[0]
                dve.wait_ge(dev_done[which], g + 1)
                if not (isinstance(i, int) and o < 1):
                    dve.wait_ge((x1_done, y_done)[which], g)
                factors(Chain(dve, factor_step[which], g, 2), d_rs[:, which, 0, :], d_rs[:, which, 1, :],
                        d_mv[:, which, :, 0], d_dev[:, which, :])

            def row_stats(ch, which, src, b):
                for j in range(J):
                    last = nc.vector.bn_stats(d_st[:, which, j, :], src[:, b, j * D:(j + 1) * D])
                ch.add(last)
                settle(dve)
                for j in range(J):
                    last = nc.vector.bn_aggr(d_mv[:, which, j, :], d_st[:, which, j, :])
                ch.add(last)

            def x_stats(i, o):
                if skip(i, o, GROUPS):
                    return
                g, k, b = at(i, o, DB)
                dve.wait_ge(x_biased, g + 1)
                row_stats(Chain(dve, x_step, g, X_STEPS), 0, d_x, b)

            def half(psum, done, used, dst, i, o):
                if skip(i, o, GROUPS):
                    return
                g, k, b = at(i, o, DB)
                dve.wait_ge(psum, g + 1)
                freed(dve, used, i, o, DB, 2)
                nc.vector.tensor_copy(dst[:, b, GROUP:2 * GROUP], bank[T_BANK[1]][:, :]).then_inc(done, 1)

            def y_stats(i, o):
                if skip(i, o, GROUPS):
                    return
                g, k, b = at(i, o, DB)
                dve.wait_ge(y_stored[b], 16 * k)
                ch = Chain(dve, y_step, g, Y_STEPS)
                for m in range(2):
                    dve.wait_ge(y_psum, 2 * g + m + 1)
                    c = slice(m * 2 * D, (m + 1) * 2 * D)
                    ch.add(nc.vector.tensor_tensor(d_y[:, b, c], bank[W_BANK[m]][:, :], d_x1[:, b, c], ALU.add))
                row_stats(ch, 1, d_y, b)

            def equal(s, i, o):
                if skip(i, o, TILES):
                    return
                t, k, b = at(i, o, EB)
                arrived(dve, s, "row_in", k, b)
                freed(dve, s["tot"], i, o, EB)
                nc.vector.tensor_scalar(e_eq[:, b, :], e_row[:, b, :], dst_f[:, bass.ds(t, 1)], None, ALU.is_equal).then_inc(s["eq"], 1)

            def row_moments(ch, b):
                ch.add(nc.vector.bn_stats(e_st[:, :], e_z[:, b, :]))
                settle(dve)
                ch.add(nc.vector.bn_aggr(e_mv[:, b, :], e_st[:, :]))

            def tile_factors(s, i, o):
                if skip(i, o, TILES):
                    return
                t, k, b = at(i, o, EB)
                dve.wait_ge(s["dev"], t + 1)
                freed(dve, s["o"], i, o, EB)
                factors(Chain(dve, s["factor"], t, 2), e_rs[:, b, 0:1], e_rs[:, b, 1:2], e_mv[:, b, 0:1], e_dev[:, b:b + 1])

            def g_rows(i, o):
                if skip(i, o, TILES):
                    return
                t, k, b = at(i, o, EB)
                dve.wait_ge(G0["deg"], t + 1)
                arrived(dve, G0, "dst_in", k, b)
                freed(dve, G0["o"], i, o, EB)
                if not (isinstance(i, int) and o < 1):
                    dve.wait_ge(G0["fin"], FIN_STEPS[0] * t)
                ch = Chain(dve, G0["fin"], t, FIN_STEPS[0])
                ch.add(nc.vector.tensor_scalar(e_nrm[:, 0:1], e_sd[:, b:b + 1], 1.0, None, ALU.max))
                ch.add(nc.vector.reciprocal(e_nrm[:, 0:1], e_nrm[:, 0:1]))
                ch.add(nc.vector.scalar_tensor_tensor(e_z[:, b, :], bank[GTOT_BANK[b % 2]][:, 0:D], e_nrm[:, 0:1], b0_all[:, :], ALU.mult, ALU.add))
                ch.add(nc.vector.tensor_tensor(e_z[:, b, :], e_z[:, b, :], e_dst[:, b, :], ALU.add))
                row_moments(ch, b)

            def first_pass(i, o):
                group_factors(1, i, o - 2)
                tile_factors(G0, i, o - 3)
                equal(G0, i, o)
                g_rows(i, o - 2)
                half(x1T_psum, x1T_dve, h_psum, d_x1T, i, o + 1)
                group_factors(0, i, o + 2)
                y_stats(i, o - 1)
                half(hT_psum, hT_dve, y_psum, d_hT, i, o)
                x_stats(i, o + 3)
            run(dve, first_pass, GROUPS, 3, 3, TILES - GROUPS)

            for l in range(2):
                s, c, m = A[l], CB[l], SM[l]

                def attend(i, o):
                    if not skip(i, o + 1, TILES):
                        t, k, b = at(i, o + 1, EB)
                        dve.wait_ge(s["T_psum"], t + 1)
                        freed(dve, s["v_psum"], i, o + 1, EB)
                        nc.vector.tensor_copy(e_atT[:, b, :], bank[3 + b % 2][:, D:D + P]).then_inc(s["aT_out"], 1)
                    if skip(i, o, TILES):
                        return
                    t, k, b = at(i, o, EB)
                    dve.wait_ge(s["k_psum"], t + 1)
                    dve.wait_ge(s["qs_out"], t + 1)
                    if not (isinstance(i, int) and o < 1):
                        dve.wait_ge(s["score"], 2 * t)
                    ch = Chain(dve, s["score"], t, 2)
                    ch.add(nc.vector.tensor_tensor(e_prod[:, :], bank[3 + b % 2][:, 0:D], e_qs[:, b, 0:D], ALU.mult))
                    ch.add(nc.vector.tensor_reduce(alpha[:, bass.ds(t * H, H)], e_prod[:, :].rearrange("p (h c) -> p h c", h=H), AX.X, ALU.add))
                    if l:
                        arrived(dve, s, "res_in", k, b)
                        nc.vector.tensor_tensor(e_qs[:, b, D:2 * D], e_qs[:, b, D:2 * D], e_res[:, b, :], ALU.add).then_inc(s["res_added"], 1)
                run(dve, attend, TILES, 0, 1)

                dve.wait_ge(s["score"], 2 * TILES)
                nc.vector.memset(alpha[0:1, :], -BIG).then_inc(m["masked"], 1)
                ch = Chain(dve, m["step"], 0, SM_STEPS)
                dve.wait_ge(m["aT"], 1)
                ch.add(nc.vector.tensor_copy(m_a[:, :], bank[7][0:TILES, :]))

                def scans(carried):
                    for h in range(H):
                        f = m_f[:, h * P:(h + 1) * P]
                        r = m_r[:, h * P:(h + 1) * P]
                        x = m_a[:, h * P:(h + 1) * P]
                        nc.vector.tensor_tensor_scan(f, m_same[:, 0, :], x, m_cin[:, h:h + 1] if carried else -BIG, ALU.min, ALU.max)
                        last = nc.vector.tensor_tensor_scan(r[:, ::-1], m_same[:, 1, ::-1], x[:, ::-1],
                                                            m_cin[:, 32 + h:33 + h] if carried else -BIG, ALU.min, ALU.max)
                    ch.add(last)
                scans(False)
                ch.add(nc.vector.tensor_copy(m_end[:, 0:H], m_f.rearrange("t (h s) -> t h s", h=H)[:, :, P - 1]))
                ch.add(nc.vector.tensor_copy(m_end[:, 32:32 + H], m_r.rearrange("t (h s) -> t h s", h=H)[:, :, 0]))
                dve.wait_ge(m["ends"], 1)
                ch.add(nc.vector.tensor_copy(m_rows[:, :], bank[0][0:64, 0:TILES]))
                fw, bw = slice(0, 32), slice(32, 64)
                ch.add(nc.vector.tensor_tensor_scan(m_scan[fw, :], m_gate[fw, 0, :], m_rows[fw, :], -BIG, ALU.min, ALU.max))
                ch.add(nc.vector.tensor_tensor_scan(m_scan[bw, ::-1], m_gate[bw, 0, ::-1], m_rows[bw, ::-1], -BIG, ALU.min, ALU.max))
                ch.add(nc.vector.memset(m_in[:, :], -BIG))
                ch.add(nc.vector.tensor_tensor(m_in[fw, 1:TILES], m_scan[fw, 0:TILES - 1], m_gate[fw, 1, 1:TILES], ALU.min))
                ch.add(nc.vector.tensor_tensor(m_in[bw, 0:TILES - 1], m_scan[bw, 1:TILES], m_gate[bw, 1, 0:TILES - 1], ALU.min))
                dve.wait_ge(m["cin"], 1)
                ch.add(nc.vector.tensor_copy(m_cin[:, :], bank[1][0:TILES, 0:64]))
                scans(True)
                ch.add(nc.vector.tensor_tensor(m_f[:, :], m_f[:, :], m_r[:, :], ALU.max))
                dve.wait_ge(m["max_psum"], 1)
                nc.vector.tensor_tensor(ex.rearrange("p (t h) -> p h t", h=H), alpha.rearrange("p (t h) -> p h t", h=H),
                                        bank[7][:, 0:H * TILES].rearrange("p (h t) -> p h t", h=H), ALU.subtract).then_inc(m["max"], 1)

                def combine(i, o):
                    equal(c, i, o + 2)
                    if l:
                        tile_factors(c, i, o - 2)
                    if skip(i, o - 1, TILES):
                        return
                    t, k, b = at(i, o - 1, EB)
                    tot = bank[b]
                    dve.wait_ge(c["tot"], t + 1)
                    if not (isinstance(i, int) and o == TILES):
                        dve.wait_ge(c["carry"], t + 2)
                    arrived(dve, c, "self_in", k, b)
                    freed(dve, c["o"], i, o - 1, EB)
                    if not (isinstance(i, int) and o <= 1):
                        dve.wait_ge(c["fin"], FIN_STEPS[1 + l] * t)
                    ch = Chain(dve, c["fin"], t, FIN_STEPS[1 + l])
                    ch.add(nc.vector.tensor_scalar(e_nrm[:, 0:H], tot[:, D:CW], SOFTMAX_EPS, None, ALU.add))
                    ch.add(nc.vector.reciprocal(e_nrm[:, 0:H], e_nrm[:, 0:H]))
                    ch.add(nc.vector.tensor_tensor(e_z[:, b, :].rearrange("p (h c) -> p h c", h=H),
                                                   tot[:, 0:D].rearrange("p (h c) -> p h c", h=H),
                                                   e_nrm[:, 0:H].rearrange("p (h o) -> p h o", o=1).to_broadcast([P, H, C]), ALU.mult))
                    ch.add(nc.vector.tensor_tensor(e_z[:, b, :], e_z[:, b, :], e_res[:, b, :], ALU.add))
                    if l:
                        row_moments(ch, b)
                run(dve, combine, TILES, 1 + l, 2)

        @block.tensor
        def _(pe):
            pe.wait_ge(ident_done, 2)
            pe.wait_ge(prep_done, 5)
            pe.wait_ge(weights_in, 16 * 11)
            pe.wait_ge(bias_moved, 16 * 4)

            def transpose_group(src, done, i, o, ready, others, before):
                if skip(i, o, GROUPS):
                    return
                g, k, b = at(i, o, DB)
                pe.wait_ge(ready, g + 1)
                n = g - before
                if not (isinstance(i, int) and not 0 <= n < GROUPS):
                    for s in others:
                        pe.wait_ge(s, n + 1)
                for kk in range(2):
                    for j in range(J):
                        last = nc.tensor.transpose(bank[T_BANK[kk]][:, j * P:(j + 1) * P],
                                                   src[:, b, j * D + kk * P:j * D + (kk + 1) * P], ident[:, :])
                last.then_inc(done, 1)

            def product(srcT, layer, done, i, o, in_a, in_d, read, before, times):
                if skip(i, o, GROUPS):
                    return
                g, k, b = at(i, o, DB)
                pe.wait_ge(in_a, g + 1)
                pe.wait_ge(in_d, g + 1)
                n = g - before
                if not (isinstance(i, int) and not 0 <= n < GROUPS):
                    pe.wait_ge(read, (n + 1) * times)
                for m in range(2):
                    for jj in range(2):
                        j = 2 * m + jj
                        dst = bank[W_BANK[m]][:, jj * D:(jj + 1) * D]
                        nc.tensor.matmul(dst, ones_bf[:, :], bias_mm[:, 2 * layer, D:2 * D], start=True, stop=False)
                        for kk in range(2):
                            last = nc.tensor.matmul(dst, srcT[:, b, kk * GROUP + j * P:kk * GROUP + (j + 1) * P],
                                                    w_qs[layer][:, kk, D:2 * D], start=False, stop=kk == 1)
                    last.then_inc(done, 1)

            def sums(s, rhs, width, tot, free, i, o):
                if skip(i, o, TILES):
                    return
                t, k, b = at(i, o, EB)
                pe.wait_ge(s["eq"], t + 1)
                pe.wait_ge(s["carry"], t + 1)
                freed(pe, s["fin"], i, o, free[0], free[1])
                nc.tensor.matmul(tot[:, 0:width], e_eq[:, b, :], rhs[:, b, 0:width], start=True, stop=True).then_inc(s["tot"], 1)

            def cols(t, b, k):
                return t[:, b, k * P:(k + 1) * P]

            def g_transposes(i, o):
                if skip(i, o, TILES):
                    return
                t, k, b = at(i, o, EB)
                arrived(pe, G0, "src_in", k, b)
                arrived(pe, G0, "attr_in", k, b)
                freed(pe, G0["T_out"], i, o, 1)
                for kk in range(4):
                    last = nc.tensor.transpose(cols_of(bank[GT_BANK], kk), cols((e_src, e_attr)[kk // 2], b, kk % 2), ident[:, :])
                last.then_inc(G0["T_psum"], 1)

            def cols_of(t, k):
                return t[:, k * P:(k + 1) * P]

            def messages(i, o):
                if skip(i, o, TILES):
                    return
                t, k, b = at(i, o, EB)
                pe.wait_ge(G0["T_out"], t + 1)
                freed(pe, G0["rhs_in"], i, o, 1)
                for kk in range(4):
                    last = nc.tensor.matmul(bank[GM_BANK][:, 0:D], cols(e_inT, b, kk), w0[:, kk, :], start=kk == 0, stop=kk == 3)
                last.then_inc(G0["M_psum"], 1)

            def first_pass(i, o):
                product(d_x1T, 0, h_psum, i, o, x1T_act, x1T_dve, y_step, 2, Y_STEPS)
                transpose_group(d_x1, x1T_psum, i, o + 1, x1_done, (hT_act, hT_dve), 2)
                g_transposes(i, o + 1)
                product(d_hT, 1, y_psum, i, o - 1, hT_act, hT_dve, h_done, -1, 1)
                transpose_group(d_h, hT_psum, i, o, h_done, (x1T_act, x1T_dve), -1)
                messages(i, o)
                sums(G0, e_rhs0, D + 1, bank[GTOT_BANK[(o - 1) % 2]], (2, FIN_STEPS[0]), i, o - 1)
            run(pe, first_pass, GROUPS, 1, 1, TILES - GROUPS)

            for l in range(2):
                s, c, m = A[l], CB[l], SM[l]

                def transposes(i, o):
                    if skip(i, o, TILES):
                        return
                    t, k, b = at(i, o, EB)
                    for n in ("src_in", "attr_in", "dst_in"):
                        arrived(pe, s, n, k, b)
                    freed(pe, s["T_out"], i, o, 2)
                    freed(pe, s["aT_out"], i, o, 2)
                    freed(pe, s["score"], i, o, 2, 2)
                    for kk in range(4):
                        nc.tensor.transpose(cols_of(bank[o % 2], kk), cols((e_src, e_dst)[kk // 2], b, kk % 2), ident[:, :])
                    nc.tensor.transpose(bank[3 + o % 2][:, D:D + P], e_attr[:, b, 0:P], ident[:, :]).then_inc(s["T_psum"], 1)

                def attend(i, o):
                    transposes(i, o + 1)
                    if skip(i, o, TILES):
                        return
                    t, k, b = at(i, o, EB)
                    q = o % 2
                    pe.wait_ge(s["T_out"], t + 1)
                    pe.wait_ge(s["aT_out"], t + 1)
                    freed(pe, s["qs_out"], i, o, 2)
                    srcT, dstT = (cols(e_inT, b, 0), cols(e_inT, b, 1)), (cols(e_inT, b, 2), cols(e_inT, b, 3))

                    def project(out_, bias, w, attr, rows):
                        nc.tensor.matmul(out_, ones_bf[:, :], bias, start=True, stop=False)
                        if attr:
                            nc.tensor.matmul(out_, e_atT[:, b, :], w_e[l][:, :], start=False, stop=False)
                        nc.tensor.matmul(out_, rows[0], w[:, 0], start=False, stop=False)
                        return nc.tensor.matmul(out_, rows[1], w[:, 1], start=False, stop=True)

                    project(bank[5 + q][:, :], bias_mm[:, 2 * l, :], w_qs[l], False, dstT).then_inc(s["qs_psum"], 1)
                    freed(pe, s["score"], i, o, 2, 2)
                    project(bank[3 + q][:, 0:D], bias_mm[:, 2 * l + 1, 0:D], w_kv[l][:, :, 0:D], True, srcT).then_inc(s["k_psum"], 1)
                    freed(pe, s["v_out"], i, o, 2)
                    project(bank[(2, 7)[q]][:, 0:D], bias_mm[:, 2 * l + 1, D:2 * D], w_kv[l][:, :, D:2 * D], True, srcT).then_inc(s["v_psum"], 1)
                run(pe, attend, TILES, 0, 1)

                pe.wait_ge(m["masked"], 1)
                pe.wait_ge(s["v_out"], TILES)
                for h in range(H):
                    last = nc.tensor.transpose(bank[7][0:TILES, h * P:(h + 1) * P], alpha.rearrange("p (t h) -> p h t", h=H)[:, h, :], ident[:, :])
                last.then_inc(m["aT"], 1)
                pe.wait_ge(m["step"], 4)
                nc.tensor.transpose(bank[0][:, 0:TILES], m_end[:, :], ident[0:TILES, 0:TILES]).then_inc(m["ends"], 1)
                pe.wait_ge(m["step"], 10)
                nc.tensor.matmul(bank[1][0:TILES, 0:64], m_in[:, :], ident[0:64, 0:64], start=True, stop=True).then_inc(m["cin"], 1)
                pe.wait_ge(m["step"], SM_STEPS)
                for h in range(H):
                    last = nc.tensor.transpose(bank[7][:, h * TILES:(h + 1) * TILES], m_f[:, h * P:(h + 1) * P], ident[0:TILES, 0:TILES])
                last.then_inc(m["max_psum"], 1)
                run(pe, lambda i, o: sums(c, e_rhs, CW, bank[o % EB], (EB, FIN_STEPS[1 + l]), i, o), TILES, 0, 0)


SPLIT_STEPS = 2 * (1 + 2 * 5)
SM_STEPS = 13
UNROLL = 4

def layout(inputs):
    pad = N

    def rows(v, fill):
        full = np.full((TILES * EPT,) + v.shape[1:], fill, v.dtype)
        full[:E] = v
        return full.reshape((TILES, EPT) + v.shape[1:])

    def attr(v):
        slots = np.zeros((TILES, P, v.shape[1]), v.dtype)
        slots[:, 1:] = rows(v, 0)
        return slots.reshape(TILES * P, v.shape[1])

    dst = rows(np.asarray(inputs["dst"]), pad)
    src = rows(np.asarray(inputs["src"]), 0)
    none = np.full((1,), -1, dst.dtype)
    after = np.concatenate([dst.reshape(-1)[1:], none]).reshape(TILES, EPT)
    first, last = dst[:, 0], dst[:, -1]
    next_first = np.concatenate([first[1:], none])
    prev_last = np.concatenate([none, last[:-1]])
    slots = np.concatenate([first[:, None], dst], 1)
    return {
        "src_slots": np.concatenate([src[:, :1], src], 1).T,
        "dst_slots": slots.T,
        "dst_next": np.concatenate([first[:, None], after], 1).T,
        "dst_rows": np.concatenate([next_first[:, None], dst], 1),
        "dst_tiles": np.concatenate([first[:, None], slots, last[:, None]], 1),
        "tile_ends": np.stack([first, last, prev_last, next_first]),
        "attr_128": attr(np.asarray(inputs["edge_attr_128"])),
        "attr_256": attr(np.asarray(inputs["edge_attr_256"])),
    }


def kernel(**inputs):
    import concourse.bacc as bacc
    from concourse import mybir as mb
    from concourse.bass_utils import run_bass_kernel_spmd

    arrays = {n: np.asarray(v) for n, v in inputs.items() if n not in ("src", "dst", "edge_attr_128", "edge_attr_256")}
    arrays.update(layout(inputs))
    arrays = {f"in_{n}": np.ascontiguousarray(v) for n, v in arrays.items()}
    nc = bacc.Bacc("TRN2", target_bir_lowering=False, num_devices=1)
    args = {n[3:]: nc.dram_tensor(n, v.shape, mb.dt.from_np(v.dtype), kind="ExternalInput").ap() for n, v in arrays.items()}
    out = nc.dram_tensor("out", (N, D), mb.dt.float32, kind="ExternalOutput").ap()
    build(nc, args, out)
    return run_bass_kernel_spmd(nc, [arrays], core_ids=[0]).results[0]["out"]
```

```python
import numpy as np
import concourse.bass as bass
import concourse.mybir as mybir
from contextlib import ExitStack

F32 = mybir.dt.float32
F32R = mybir.dt.float32r
BF16 = mybir.dt.bfloat16
I32 = mybir.dt.int32
ALU = mybir.AluOpType
ACT = mybir.ActivationFunctionType
AX = mybir.AxisListType

P = 128
N, D, ED, H, E = 50000, 256, 128, 4, 12500
C = D // H
EPT = P - 1
EB = 4
TILES = EB * -(-E // (EB * EPT))
J = 4
GROUP = P * J
GROUPS = -(-N // GROUP)
DB = 4
LN_EPS = 1e-5
SOFTMAX_EPS = 1e-16
BIG = float(2 ** 100)
CW = D + H
HI, LO = 0, 1
PASSES = ((LO, HI), (HI, LO), (HI, HI))


def build(nc, a, out):
    ctx = ExitStack()
    with ctx:
        def sb(name, shape, dt=F32):
            return ctx.enter_context(nc.sbuf_tensor(name, shape, dt))

        def pb(name):
            return ctx.enter_context(nc.psum_tensor(name, [P, 512], F32))

        def sem(name):
            return ctx.enter_context(nc.semaphore(name))

        def sems(name, n):
            return [sem(f"{name}{i}") for i in range(n)]

        x1_table = nc.dram_tensor("x1_table", [N, D], F32).ap()
        h_table = nc.dram_tensor("h_table", [N, D], F32).ap()
        x1_spill = nc.dram_tensor("x1_spill", [TILES, P, D], F32).ap()
        self_spill = [nc.dram_tensor(f"self_spill{l}", [TILES, P, D], F32).ap() for l in range(2)]

        ident = sb("ident", [P, P])
        ones_bf = sb("ones_bf", [P, P], BF16)
        w0 = sb("w0", [P, 2, 4, D], F32R)
        w_qs = [sb(f"w_qs{l}", [P, 2, 2, 2 * D], F32R) for l in range(2)]
        w_kv = [sb(f"w_kv{l}", [P, 2, 2, 2 * D], F32R) for l in range(2)]
        w_e = [sb(f"w_e{l}", [P, 2, 1, D], F32R) for l in range(2)]
        b0_all = sb("b0_all", [P, D])
        bias_mm = sb("bias_mm", [P, 4, 2 * D], BF16)
        src_idx = sb("src_idx", [P, TILES], I32)
        dst_idx = sb("dst_idx", [P, TILES], I32)
        dst_next = sb("dst_next", [P, TILES], I32)
        dst_f = sb("dst_f", [P, TILES])
        last_idx = sb("last_idx", [P, TILES], I32)
        alpha = sb("alpha", [P, TILES * H])
        ex = sb("ex", [P, TILES * H])

        GD = J * D
        with ExitStack() as dense_space:
            def dense_buf(name, shape, dt=F32):
                return dense_space.enter_context(nc.sbuf_tensor(name, [P] + shape, dt))
            d_x, d_x1, d_h, d_y = (dense_buf(n, [DB, GD]) for n in ("d_x", "d_x1", "d_h", "d_y"))
            d_x1T, d_hT = (dense_buf(n, [2, 2, GD], F32R) for n in ("d_x1T", "d_hT"))
        assert (4 * DB + 2 * 4) * GD <= TILES * D
        vals = sb("vals", [P, TILES * D])

        def early(t, lo, shape, names, **sizes):
            n = int(np.prod(shape))
            return t.rearrange("p b n -> p (b n)")[:, lo:lo + n].rearrange(f"p ({names}) -> p {names}", **sizes)
        bias_row = early(d_h, 0, (6, 2 * D), "r n", r=6)[0:1]
        bias_hi = d_y.rearrange("p b n -> p (b n)")[0:1, 0:12 * D].bitcast(BF16).rearrange(
            "o (i r n) -> o i r n", i=4, r=3)
        raw_weights = [(w_qs[0], D, "L1_gnn_Ws1", early(d_h, 12 * D, (2, D), "k n", k=2)),
                       (w_qs[1], D, "L1_gnn_Ws2", early(d_h, 14 * D, (2, D), "k n", k=2)),
                       (w0, 0, "L0_gnn_weights", early(d_y, 12 * D, (4, D), "k n", k=4))]
        at_column = 0
        for l in range(2):
            for t, col, n, chunks in ((w_qs[l], 0, "Wq", 2), (w_kv[l], 0, "Wk", 2), (w_kv[l], D, "Wv", 2), (w_e[l], 0, "We", 1)):
                raw_weights.append((t, col, f"L1_gnn_{n}{l + 1}", early(d_x1, at_column, (chunks, D), "k n", k=chunks)))
                at_column += chunks * D

        d_st = sb("d_st", [P, 2, J, 6])
        d_mv = sb("d_mv", [P, 2, 2, J, 2])
        d_dev = sb("d_dev", [P, 2, J])
        d_rs = sb("d_rs", [P, 2, 2, J])

        e_src = sb("e_src", [P, EB, D])
        e_dst = sb("e_dst", [P, EB, D])
        e_res = sb("e_res", [P, EB, D])
        e_attr = sb("e_attr", [P, EB, D])
        e_inT = sb("e_inT", [P, 2, 2, 4 * P], F32R)
        e_atT = sb("e_atT", [P, 2, 2, P], F32R)
        zero_row = sb("zero_row", [1, CW])
        ln_eps = sb("ln_eps", [P, 1])
        e_rhs = sb("e_rhs", [P, EB, CW])
        e_row = sb("e_row", [P, EB, P], I32)
        e_eq = sb("e_eq", [P, EB, P])
        e_prod = sb("e_prod", [P, D])
        e_zo = sb("e_zo", [P, 2, EB, D])
        e_z, e_o = e_zo[:, 0], e_zo[:, 1]
        e_qs = e_zo.rearrange("p r b d -> p (r b d)").rearrange("p (b n) -> p b n", b=EB)
        e_st = sb("e_st", [P, 6])
        e_mv = sb("e_mv", [P, EB, 2])
        e_sd = sb("e_sd", [P, EB])
        e_dev = sb("e_dev", [P, EB])
        e_rs = sb("e_rs", [P, EB, 2])
        e_nrm = sb("e_nrm", [P, 4])
        e_sx = [sb(f"e_sx{i}", [P, 1], I32) for i in range(EB)]
        e_rx = [sb(f"e_rx{i}", [P, 1], I32) for i in range(EB)]
        e_dx = [sb(f"e_dx{i}", [P, 1], I32) for i in range(EB)]
        e_lx = [sb(f"e_lx{i}", [P, 1], I32) for i in range(EB)]

        m_dst = sb("m_dst", [TILES, P + 2], I32)
        m_same = sb("m_same", [TILES, 2, P])
        m_a, m_f = (e_src.rearrange("p b d -> p (b d)")[0:TILES, i * H * P:(i + 1) * H * P] for i in range(2))
        m_r = e_attr.rearrange("p b d -> p (b d)")[0:TILES, 0:H * P]
        m_end = sb("m_end", [TILES, P])
        m_edge = sb("m_edge", [64, 4, TILES], I32)
        m_gate = sb("m_gate", [64, 2, TILES])
        m_rows = sb("m_rows", [64, TILES])
        m_scan = sb("m_scan", [64, TILES])
        m_in = sb("m_in", [64, TILES])
        m_cin = sb("m_cin", [TILES, 64])

        bank = [pb(f"bank{i}") for i in range(8)]
        T_BANK, W_BANK = (0, 1), (2, 3)
        GT_BANK, GM_BANK, GTOT_BANK = 4, 5, (6, 7)

        weight_in = [sem(f"weight_in{i}") for i in range(4)]
        weights_hi = sem("weights_hi")
        weights_lo = sem("weights_lo")
        biases_in = sem("biases_in")
        b0_in = sem("b0_in")
        index_in = sem("index_in")
        ends_in = sem("ends_in")
        ident_done = sem("ident_done")
        pads_done = sem("pads_done")
        prep_done = sem("prep_done")
        split_step = sem("split_step")
        bias_moved = sem("bias_moved")

        x_loaded = sems("x_loaded", DB)
        x1_stored = sems("x1_stored", DB)
        h_stored = sems("h_stored", DB)
        y_stored = sems("y_stored", DB)
        x_biased = sem("x_biased")
        x_step = sem("x_step")
        y_step = sem("y_step")
        dev_done = sems("dev_done", 2)
        factor_step = sems("factor_step", 2)
        x1_done = sem("x1_done")
        x1T_psum = sem("x1T_psum")
        x1T_hi = sem("x1T_hi")
        x1T_lo = sem("x1T_lo")
        h_psum = sem("h_psum")
        h_done = sem("h_done")
        hT_psum = sem("hT_psum")
        hT_hi = sem("hT_hi")
        hT_lo = sem("hT_lo")
        y_psum = sem("y_psum")
        y_done = sem("y_done")

        slot = {n: sems(n, EB) for n in ("src_in", "dst_in", "attr_in", "row_in", "res_in", "self_in", "spilled", "scattered")}
        USES = TILES // EB

        def edge_sems(ph, counts, **before):
            d = {n: sem(f"{ph}_{n}") for n in counts}
            d["before"] = before
            return d
        G0 = edge_sems("g", ("src_in_ix", "dst_in_ix", "dst_biased", "T_psum", "T_hi", "T_lo", "M_psum", "rhs_in", "carry", "eq", "tot", "deg",
                             "fin", "dev", "factor", "o"), src_in=0, dst_in=0, attr_in=0, row_in=0, spilled=0)
        R0 = edge_sems("r", ("scattered_ix",), self_in=0, scattered=0)
        A = [edge_sems(f"a{l}", ("src_in_ix", "dst_in_ix", "T_psum", "T_hi", "T_lo", "qs_psum", "k_psum", "v_psum",
                                 "qs_out", "v_out", "score") + (("res_in_ix", "res_added") if l else ()),
                       src_in=1 + l, dst_in=1 + l, attr_in=1 + l, res_in=0, spilled=1 + l) for l in range(2)]
        CB = [edge_sems(f"c{l}", ("scattered_ix", "weighed", "carry", "eq", "tot", "fin", "o") + (("dev", "factor") if l else ()),
                        row_in=1 + l, self_in=1 + l, scattered=1 + l) for l in range(2)]
        SM = [edge_sems(f"s{l}", ("masked", "aT", "step", "ends", "cin", "max_psum", "max", "exp")) for l in range(2)]
        settled = sem("settled")
        m_step = sem("m_step")
        idx_step = sem("idx_step")

        def at(i, o, n):
            return n * i + o, i + o // n, o % n

        def settle(eng):
            eng.sem_inc(settled)

        def skip(i, o, total):
            return isinstance(i, int) and not 0 <= o < total

        def freed(eng, s, i, o, n, times=1):
            if isinstance(i, int) and o < n:
                return
            eng.wait_ge(s, (UNROLL * i + o - n + 1) * times)

        def arrived(eng, s, what, k, b):
            eng.wait_ge(slot[what][b], 16 * (k + s["before"][what] * USES + 1))

        def over(eng, s, what, k, b):
            eng.wait_ge(slot[what][b], 16 * (k + s["before"][what] * USES))

        def all_over(eng, s, what):
            for b in range(EB):
                eng.wait_ge(slot[what][b], 16 * USES * (s["before"][what] + 1))

        def run(eng, f, total, back, ahead, more=0):
            start = back + UNROLL
            rounds = (total - ahead - start) // UNROLL
            for o in range(-ahead, start):
                f(0, o)
            with eng.Fori(0, rounds) as i:
                for o in range(start, start + UNROLL):
                    f(i, o)
            for o in range(start + rounds * UNROLL, total + more + back):
                f(0, o)

        class Chain:
            def __init__(self, eng, s, item, steps):
                self.eng, self.s, self.base, self.steps, self.j = eng, s, item * steps, steps, 0

            def add(self, ins):
                self.j += 1
                ins.then_inc(self.s, 1)
                if self.j < self.steps:
                    self.eng.wait_ge(self.s, self.base + self.j)

        def transposed(o):
            return (e_inT, bank[o % 2][:, :]), (e_atT, bank[3 + o % 2][:, D:D + P])

        class Steps(Chain):
            def start(self):
                if self.j:
                    self.eng.wait_ge(self.s, self.base + self.j)

            def end(self, ins):
                self.j += 1
                ins.then_inc(self.s, 1)

        X_STEPS, Y_STEPS = 2, 4
        FIN_STEPS = (5, 3, 5)

        def dense_base(i, o):
            return N - GROUP if isinstance(i, int) and o == GROUPS - 1 else GROUP * (DB * i + o)

        def node_rows(t, base, lo=0):
            return t[bass.ds(base + lo * J, (P - lo) * J), :].rearrange("(p j) d -> p (j d)", j=J)

        def tile_of(t, n):
            return t[bass.ds(n, 1), :, :].rearrange("o p d -> (o p) d")

        def all_uses(b, total):
            return 16 * len(range(b, total, DB))

        block = ctx.enter_context(nc.Block())

        @block.sync
        def _(sp):
            sp.dma_start(b0_all[:, :], a["L0_gnn_h_bias"].rearrange("(o n) -> o n", o=1).to_broadcast([P, D])).then_inc(b0_in, 16)

            def load_x(i, o):
                if skip(i, o, GROUPS):
                    return
                g, k, b = at(i, o, DB)
                freed(sp, x1_done, i, o, DB)
                sp.dma_start(d_x[:, b, :], node_rows(a["x"], dense_base(i, o))).then_inc(x_loaded[b], 16)
            for o in range(2):
                load_x(0, o)
            def load_weight(n):
                t, col, name, raw = raw_weights[n]
                sp.dma_start(raw, a[name].rearrange("(k p) n -> p k n", p=P)).then_inc(weight_in[min(n, 3)], 16)
            for n in range(2):
                load_weight(n)
            for l in range(2):
                for r, b, o in ((0, "bq", 0), (0, "bs", D), (1, "bk", 0), (1, "bv", D), (2, "be", 0), (2, "be", D)):
                    sp.dma_start(bias_row[0:1, 3 * l + r, o:o + D],
                                 a[f"L1_gnn_{b}{l + 1}"].rearrange("(o n) -> o n", o=1)).then_inc(biases_in, 16)
            for n in range(2, len(raw_weights)):
                load_weight(n)
            for t, s in ((src_idx, "src_slots"), (dst_idx, "dst_slots"), (dst_next, "dst_next")):
                sp.dma_start(t[:, :], a[s]).then_inc(index_in, 16)
            sp.dma_start(m_dst[:, :], a["dst_tiles"]).then_inc(ends_in, 16)
            for r in range(4):
                sp.dma_start(m_edge[:, r, :], a["tile_ends"][r:r + 1, :].to_broadcast([64, TILES])).then_inc(ends_in, 16)
            sp.wait_ge(split_step, SPLIT_STEPS)
            sp.wait_ge(prep_done, 1)
            for i in range(4):
                sp.dma_start(bias_mm[0:3, i, :], bias_hi[0:1, i, :, :]).then_inc(bias_moved, 16)

            def store(i, o, src, table, done, stored, times=1):
                if skip(i, o, GROUPS):
                    return
                g, k, b = at(i, o, DB)
                sp.wait_ge(done, (g + 1) * times)
                lo = (GROUPS * GROUP - N) // J if isinstance(i, int) and o == GROUPS - 1 else 0
                sp.dma_start(node_rows(table, dense_base(i, o), lo), src[lo:, b, :]).then_inc(stored[b], 16)

            def load_row(s, i, o):
                if skip(i, o, TILES):
                    return
                t, k, b = at(i, o, EB)
                freed(sp, s["eq"], i, o, EB)
                settle(sp)
                sp.dma_start(e_row[:, b, :], a["dst_rows"][bass.ds(t, 1), :].to_broadcast([P, P])).then_inc(slot["row_in"][b], 16)

            def load_attr(s, attr, width, i, o):
                if skip(i, o, TILES):
                    return
                t, k, b = at(i, o, EB)
                freed(sp, s["T_psum"], i, o, EB)
                sp.dma_start(e_attr[:, b, 0:width], attr[bass.ds(t * P, P), :]).then_inc(slot["attr_in"][b], 16)

            def spill(s, done, src, table, i, o):
                if skip(i, o, TILES):
                    return
                t, k, b = at(i, o, EB)
                sp.wait_ge(done, t + 1)
                sp.dma_start(tile_of(table, t), src(b)).then_inc(slot["spilled"][b], 16)

            def first_pass(i, o):
                load_attr(G0, a["attr_256"], 2 * ED, i, o + 3)
                load_row(G0, i, o + 2)
                if not (isinstance(i, int) and o + 5 < 2):
                    load_x(i, o + 5)
                store(i, o, d_h, h_table, h_done, h_stored, 2)
                store(i, o + 2, d_x1, x1_table, x1_done, x1_stored)
                store(i, o - 2, d_y, out, y_done, y_stored)
                spill(G0, G0["o"], lambda b: e_o[:, b, :], x1_spill, i, o - 3)
            run(sp, first_pass, GROUPS, 3, 5, TILES - GROUPS)

            all_over(sp, G0, "spilled")

            def reload(i, o):
                t, k, b = at(i, o, EB)
                if not (isinstance(i, int) and o < EB):
                    over(sp, R0, "scattered", k, b)
                sp.dma_start(e_res[:, b, :], tile_of(x1_spill, t)).then_inc(slot["self_in"][b], 16)
            run(sp, reload, TILES, 0, 0)

            sp.wait_ge(G0["T_psum"], TILES)
            for l in range(2):
                def attend(i, o):
                    load_attr(A[l], a["attr_128"], ED, i, o + 3)
                    spill(A[l], A[l]["res_added" if l else "qs_out"], lambda b: e_qs[:, b, D:2 * D], self_spill[l], i, o)
                run(sp, attend, TILES, 0, 3)
                all_over(sp, A[l], "spilled")

                def combine(i, o):
                    t, k, b = at(i, o, EB)
                    load_row(CB[l], i, o)
                    freed(sp, CB[l]["fin"], i, o, EB, FIN_STEPS[1 + l])
                    sp.dma_start(e_res[:, b, :], tile_of(self_spill[l], t)).then_inc(slot["self_in"][b], 16)
                if l == 0:
                    all_over(sp, R0, "scattered")
                run(sp, combine, TILES, 0, 0)

        @block.gpsimd
        def _(pool):
            nc.gpsimd.memset(ident[:, :], 0.0).then_inc(ident_done, 1)
            pool.wait_ge(ident_done, 1)
            nc.gpsimd.affine_select(out=ident[:, :], in_=ident[:, :], compare_op=ALU.not_equal, fill=1.0,
                                    base=0, pattern=[[-1, P]], channel_multiplier=1).then_inc(ident_done, 1)
            for t in (e_src, e_dst):
                nc.gpsimd.memset(t[:, :, :], 0.0).then_inc(pads_done, 1)
            pool.wait_ge(b0_in, 16)

            def bias(i, o):
                if skip(i, o, GROUPS):
                    return
                g, k, b = at(i, o, DB)
                pool.wait_ge(x_loaded[b], 16 * k + 16)
                v = d_x[:, b, :].rearrange("p (j d) -> p j d", j=J)
                nc.gpsimd.tensor_tensor(v, v, b0_all[:, None, :].to_broadcast([P, J, D]), ALU.add).then_inc(x_biased, 1)

            def number(s, what, index, ix, i, o):
                if skip(i, o, TILES):
                    return
                t, k, b = at(i, o, EB)
                over(pool, s, what, k, b)
                settle(pool)
                nc.gpsimd.tensor_copy(ix[b][:, :], index[:, bass.ds(t, 1)]).then_inc(s[what + "_ix"], 1)

            def gather(s, what, buf, table, index, ix, free, i, o):
                number(s, what, index, ix, i, o + 1)
                if skip(i, o, TILES):
                    return
                t, k, b = at(i, o, EB)
                freed(pool, free[0], i, o, EB, free[1])
                pool.wait_ge(s[what + "_ix"], t + 1)
                settle(pool)
                nc.gpsimd.indirect_dma_start(out=buf[:, b, :], out_offset=None, in_=table,
                                             in_offset=bass.IndirectOffsetOnAxis(ap=ix[b][:, :], axis=0),
                                             bounds_check=N - 1, oob_is_err=False).then_inc(slot[what][b], 16)

            def scatter(s, table, rows, ready, i, o):
                number(s, "scattered", last_idx, e_lx, i, o + 1)
                if skip(i, o, TILES):
                    return
                t, k, b = at(i, o, EB)
                pool.wait_ge(s["scattered_ix"], t + 1)
                ready(t, k, b)
                settle(pool)
                nc.gpsimd.indirect_dma_start(out=table, out_offset=bass.IndirectOffsetOnAxis(ap=e_lx[b][:, :], axis=0),
                                             in_=rows[:, b, :], in_offset=None,
                                             bounds_check=N - 1, oob_is_err=False).then_inc(slot["scattered"][b], 16)

            def bias_dst(i, o):
                if skip(i, o, TILES):
                    return
                t, k, b = at(i, o, EB)
                arrived(pool, G0, "dst_in", k, b)
                nc.gpsimd.tensor_tensor(e_dst[:, b, :], e_dst[:, b, :], b0_all[:, :], ALU.add).then_inc(G0["dst_biased"], 1)

            def first_pass(i, o):
                if isinstance(i, int) and o == -4:
                    pool.wait_ge(pads_done, 2)
                    pool.wait_ge(index_in, 48)
                    pool.wait_ge(idx_step, 3)
                bias(i, o + 4)
                bias_dst(i, o - 1)
                gather(G0, "src_in", e_src, a["x"], src_idx, e_sx, (G0["T_psum"], 1), i, o + 3)
                gather(G0, "dst_in", e_dst, a["x"], dst_idx, e_dx, (G0["fin"], FIN_STEPS[0]), i, o + 1)
            run(pool, first_pass, GROUPS, 1, 4, TILES - GROUPS)

            for b in range(DB):
                for stored in (x1_stored, h_stored, y_stored):
                    pool.wait_ge(stored[b], all_uses(b, GROUPS))
            run(pool, lambda i, o: scatter(R0, x1_table, e_res, lambda t, k, b: arrived(pool, R0, "self_in", k, b), i, o),
                TILES, 0, 1)
            all_over(pool, R0, "scattered")
            for l in range(2):
                table, residual = ((x1_table, None), (h_table, x1_table))[l]

                def attend(i, o):
                    gather(A[l], "src_in", e_src, table, src_idx, e_sx, (A[l]["T_psum"], 1), i, o)
                    gather(A[l], "dst_in", e_dst, table, dst_idx, e_dx, (A[l]["T_psum"], 1), i, o)
                    if residual is not None:
                        gather(A[l], "res_in", e_res, residual, dst_idx, e_rx, (A[l]["res_added"], 1), i, o - 2)
                run(pool, attend, TILES, 2 * l, 1)
                pool.wait_ge(SM[l]["exp"], 1)

                def weigh(i, o):
                    if skip(i, o, TILES):
                        return
                    t, k, b = at(i, o, EB)
                    freed(pool, CB[l]["tot"], i, o, EB)
                    w = ex[:, bass.ds(t * H, H)]
                    settle(pool)
                    nc.gpsimd.tensor_copy(e_rhs[:, b, D:CW], w)
                    nc.gpsimd.tensor_tensor(e_rhs[:, b, 0:D].rearrange("p (h c) -> p h c", h=H),
                                            vals[:, bass.ds(t * D, D)].rearrange("p (h c) -> p h c", h=H),
                                            w.rearrange("p (h o) -> p h o", o=1).to_broadcast([P, H, C]),
                                            ALU.mult).then_inc(CB[l]["weighed"], 1)

                def combine(i, o):
                    weigh(i, o + 3)
                    scatter(CB[l], out if l else h_table, e_o, lambda t, k, b: pool.wait_ge(CB[l]["o"], t + 1), i, o - 3 - 2 * l)
                run(pool, combine, TILES, 3 + 2 * l, 3)
                all_over(pool, CB[l], "scattered")

        @block.scalar
        def _(act):
            def norm_rows(which, i, o):
                if skip(i, o, GROUPS):
                    return
                g, k, b = at(i, o, DB)
                act.wait_ge(factor_step[which], 2 * g + 2)
                if which == 0:
                    act.wait_ge(x1_stored[b], 16 * k)
                    freed(act, y_step, i, o, DB, Y_STEPS)
                src, dst = (d_x, d_x1) if which == 0 else (d_y, d_y)
                for j in range(J):
                    last = nc.scalar.activation(dst[:, b, j * D:(j + 1) * D], src[:, b, j * D:(j + 1) * D], ACT.Identity,
                                                bias=d_rs[:, which, 1, j:j + 1], scale=d_rs[:, which, 0, j:j + 1])
                last.then_inc((x1_done, y_done)[which], 1)

            def deviations(which, i, o):
                if skip(i, o, GROUPS):
                    return
                g = at(i, o, DB)[0]
                steps = (X_STEPS, Y_STEPS)[which]
                act.wait_ge((x_step, y_step)[which], steps * (g + 1))
                if not (isinstance(i, int) and o < 1):
                    act.wait_ge(factor_step[which], 2 * g)
                nc.scalar.activation(d_dev[:, which, :], d_mv[:, which, o % 2, :, 1], ACT.Sqrt, bias=ln_eps[:, 0:1]).then_inc(dev_done[which], 1)

            def relu_h(i, o):
                if skip(i, o, GROUPS):
                    return
                g, k, b = at(i, o, DB)
                act.wait_ge(h_stored[b], 16 * k)
                for m in range(2):
                    act.wait_ge(h_psum, 2 * g + m + 1)
                    nc.scalar.activation(d_h[:, b, m * 2 * D:(m + 1) * 2 * D], bank[W_BANK[m]][:, :], ACT.Relu).then_inc(h_done, 1)

            def high_parts(psum, done, used, dst, i, o):
                if skip(i, o, GROUPS):
                    return
                g, k, b = at(i, o, DB)
                act.wait_ge(psum, g + 1)
                freed(act, used, i, o, 2, 2)
                for kk in range(2):
                    nc.scalar.activation(dst[:, b % 2, HI, kk * GROUP:(kk + 1) * GROUP], bank[T_BANK[kk]][:, :], ACT.Copy).then_inc(done, 1)

            def rows_high(s, used, src, i, o):
                if skip(i, o, TILES):
                    return
                t, k, b = at(i, o, EB)
                act.wait_ge(s["T_psum"], t + 1)
                freed(act, s[used], i, o, 2)
                for dst, psum in src:
                    last = nc.scalar.activation(dst[:, b % 2, HI, :], psum, ACT.Copy)
                last.then_inc(s["T_hi"], 1)

            def carry(s, below, rhs, width, tot, i, o):
                t, k, b = at(i, o, EB)
                act.wait_ge(below, t + 1)
                if isinstance(i, int) and o == 0:
                    src = zero_row[0:1, 0:width]
                else:
                    act.wait_ge(s["tot"], t)
                    src = tot[0:1, 0:width]
                nc.scalar.activation(rhs[0:1, b, 0:width], src, ACT.Copy).then_inc(s["carry"], 1)

            def deviation(s, steps, i, o):
                if skip(i, o, TILES):
                    return
                t, k, b = at(i, o, EB)
                act.wait_ge(s["fin"], steps * (t + 1))
                freed(act, s["factor"], i, o, EB, 2)
                nc.scalar.activation(e_dev[:, b:b + 1], e_mv[:, b, 1:2], ACT.Sqrt, bias=ln_eps[:, 0:1]).then_inc(s["dev"], 1)

            def finish(s, what, relu, i, o):
                if skip(i, o, TILES):
                    return
                t, k, b = at(i, o, EB)
                if relu:
                    act.wait_ge(s["fin"], FIN_STEPS[1] * (t + 1))
                else:
                    act.wait_ge(s["factor"], 2 * (t + 1))
                over(act, s, what, k, b)
                if relu:
                    nc.scalar.activation(e_o[:, b, :], e_z[:, b, :], ACT.Relu).then_inc(s["o"], 1)
                else:
                    nc.scalar.activation(e_o[:, b, :], e_z[:, b, :], ACT.Identity,
                                         bias=e_rs[:, b, 1:2], scale=e_rs[:, b, 0:1]).then_inc(s["o"], 1)

            def g_operand(i, o):
                if skip(i, o, TILES):
                    return
                t, k, b = at(i, o, EB)
                act.wait_ge(G0["M_psum"], t + 1)
                freed(act, G0["tot"], i, o, EB)
                nc.scalar.activation(e_rhs[:, b, 0:D], bank[GM_BANK][:, 0:D], ACT.Copy).then_inc(G0["rhs_in"], 1)
                carry(G0, G0["rhs_in"], e_rhs, D + 1, bank[GTOT_BANK[(b + 1) % 2]], i, o)

            def g_degree(i, o):
                if skip(i, o, TILES):
                    return
                t, k, b = at(i, o, EB)
                act.wait_ge(G0["tot"], t + 1)
                freed(act, G0["fin"], i, o, EB, FIN_STEPS[0])
                nc.scalar.activation(e_sd[:, b:b + 1], bank[GTOT_BANK[b % 2]][:, D:D + 1], ACT.Sqrt).then_inc(G0["deg"], 1)

            def first_pass(i, o):
                g_operand(i, o - 1)
                g_degree(i, o - 2)
                deviations(0, i, o + 2)
                relu_h(i, o)
                deviations(1, i, o - 2)
                high_parts(x1T_psum, x1T_hi, h_psum, d_x1T, i, o + 1)
                rows_high(G0, "M_psum", ((e_inT, bank[GT_BANK][:, :]),), i, o + 1)
                deviation(G0, FIN_STEPS[0], i, o - 3)
                norm_rows(0, i, o + 2)
                high_parts(hT_psum, hT_hi, y_psum, d_hT, i, o)
                norm_rows(1, i, o - 2)
                finish(G0, "spilled", False, i, o - 3)
            for n, (t, col, name, raw) in enumerate(raw_weights):
                act.wait_ge(weight_in[min(n, 3)], 16 if n < 3 else 16 * (len(raw_weights) - 3))
                nc.scalar.activation(t[:, HI, :, col:col + D], raw, ACT.Copy).then_inc(weights_hi, 1)
            act.wait_ge(weights_lo, len(raw_weights))
            act.wait_ge(prep_done, 5)
            run(act, first_pass, GROUPS, 3, 2, TILES - GROUPS)

            for l in range(2):
                s, c = A[l], CB[l]

                def attend(i, o):
                    rows_high(s, "v_psum", transposed(o + 1), i, o + 1)
                    if skip(i, o, TILES):
                        return
                    t, k, b = at(i, o, EB)
                    act.wait_ge(s["qs_psum"], t + 1)
                    freed(act, s["score"], i, o, EB, 2)
                    over(act, s, "spilled", k, b)
                    nc.scalar.activation(e_qs[:, b, :], bank[5 + b % 2][:, :], ACT.Copy).then_inc(s["qs_out"], 1)
                    act.wait_ge(s["v_psum"], t + 1)
                    settle(act)
                    nc.scalar.activation(vals[:, bass.ds(t * D, D)], bank[(2, 7)[b % 2]][:, 0:D], ACT.Copy).then_inc(s["v_out"], 1)
                run(act, attend, TILES, 0, 1)

                act.wait_ge(SM[l]["max"], 1)
                nc.scalar.activation(ex[:, :], ex[:, :], ACT.Exp, scale=float(C) ** -0.5).then_inc(SM[l]["exp"], 1)

                def combine(i, o):
                    if not skip(i, o, TILES):
                        carry(c, c["weighed"], e_rhs, CW, bank[(o - 1) % EB], i, o)
                    if l:
                        deviation(c, FIN_STEPS[2], i, o - 3)
                    finish(c, "scattered", l == 0, i, o - 2 - 2 * l)
                run(act, combine, TILES, 2 + 2 * l, 0)

        @block.vector
        def _(dve):
            nc.vector.memset(bias_mm[:, :, :], 0.0).then_inc(prep_done, 1)
            nc.vector.memset(zero_row[:, :], 0.0).then_inc(prep_done, 1)
            nc.vector.memset(ln_eps[:, :], LN_EPS).then_inc(prep_done, 1)
            nc.vector.memset(e_rhs[:, :, :], 1.0).then_inc(prep_done, 1)
            nc.vector.memset(ones_bf[:, :], 1.0).then_inc(prep_done, 1)

            ch = Chain(dve, split_step, 0, SPLIT_STEPS)
            dve.wait_ge(biases_in, 16 * 12)
            for l in range(2):
                r = bias_row[0:1, 3 * l:3 * l + 3, :]
                ch.add(nc.vector.tensor_tensor(r[:, 1, :], r[:, 1, :], r[:, 2, :], ALU.add))
                for m in range(2):
                    for part in range(3):
                        ch.add(nc.vector.tensor_copy(bias_hi[0:1, 2 * l + m, part, :], r[:, m, :]))
                        if part < 2:
                            ch.add(nc.vector.tensor_tensor(r[:, m, :], r[:, m, :], bias_hi[0:1, 2 * l + m, part, :], ALU.subtract))

            for n, (t, col, name, raw) in enumerate(raw_weights):
                dve.wait_ge(weights_hi, n + 1)
                nc.vector.tensor_tensor(t[:, LO, :, col:col + D], raw, t[:, HI, :, col:col + D].bitcast(F32),
                                        ALU.subtract).then_inc(weights_lo, 1)

            dve.wait_ge(index_in, 48)
            ch = Chain(dve, idx_step, 0, 3)
            ch.add(nc.vector.tensor_copy(dst_f[:, :], dst_idx[:, :]))
            ch.add(nc.vector.tensor_tensor(last_idx[:, :], dst_next[:, :], dst_idx[:, :], ALU.is_equal))
            ch.add(nc.vector.scalar_tensor_tensor(last_idx[:, :], last_idx[:, :], float(N), dst_idx[:, :], ALU.mult, ALU.add))

            dve.wait_ge(ends_in, 16 * 5)
            ch = Chain(dve, m_step, 0, 13)
            for r, lo in ((0, 0), (1, 2)):
                ch.add(nc.vector.tensor_tensor(m_same[:, r, :], m_dst[:, 1:P + 1], m_dst[:, lo:lo + P], ALU.is_equal))
                ch.add(nc.vector.tensor_scalar(m_same[:, r, :], m_same[:, r, :], 2 * BIG, -BIG, ALU.mult, ALU.add))
            first, last, prev_last, next_first = (m_edge[:, r, :] for r in range(4))
            for g, x, y in ((0, last, prev_last), (1, first, prev_last)):
                ch.add(nc.vector.tensor_tensor(m_gate[0:32, g, :], x[0:32], y[0:32], ALU.is_equal))
                ch.add(nc.vector.tensor_scalar(m_gate[0:32, g, :], m_gate[0:32, g, :], 2 * BIG, -BIG, ALU.mult, ALU.add))
            for g, x, y in ((0, first, next_first), (1, last, next_first)):
                ch.add(nc.vector.tensor_tensor(m_gate[32:64, g, :], x[32:64], y[32:64], ALU.is_equal))
                ch.add(nc.vector.tensor_scalar(m_gate[32:64, g, :], m_gate[32:64, g, :], 2 * BIG, -BIG, ALU.mult, ALU.add))
            ch.add(nc.vector.memset(m_end[:, :], 0.0))

            def factors(ch, rs_scale, rs_bias, mean, deviation):
                ch.add(nc.vector.reciprocal(rs_scale, deviation))
                ch.add(nc.vector.scalar_tensor_tensor(rs_bias, mean, -1.0, rs_scale, ALU.mult, ALU.mult))

            def group_factors(which, i, o):
                if skip(i, o, GROUPS):
                    return
                g = at(i, o, DB)[0]
                dve.wait_ge(dev_done[which], g + 1)
                if not (isinstance(i, int) and o < 1):
                    dve.wait_ge((x1_done, y_done)[which], g)
                factors(Chain(dve, factor_step[which], g, 2), d_rs[:, which, 0, :], d_rs[:, which, 1, :],
                        d_mv[:, which, o % 2, :, 0], d_dev[:, which, :])

            def row_stats(ch, which, src, b):
                for j in range(J):
                    last = nc.vector.bn_stats(d_st[:, which, j, :], src[:, b, j * D:(j + 1) * D])
                ch.add(last)
                settle(dve)
                for j in range(J):
                    last = nc.vector.bn_aggr(d_mv[:, which, b % 2, j, :], d_st[:, which, j, :])
                ch.add(last)

            def x_stats(i, o):
                if skip(i, o, GROUPS):
                    return
                g, k, b = at(i, o, DB)
                dve.wait_ge(x_biased, g + 1)
                if not (isinstance(i, int) and o < 1):
                    dve.wait_ge(x_step, X_STEPS * g)
                freed(dve, factor_step[0], i, o, 2, 2)
                row_stats(Chain(dve, x_step, g, X_STEPS), 0, d_x, b)

            def low_parts(psum_hi, done, used, dst, i, o):
                if skip(i, o, GROUPS):
                    return
                g, k, b = at(i, o, DB)
                freed(dve, used, i, o, 2, 2)
                for kk in range(2):
                    dve.wait_ge(psum_hi, 2 * g + kk + 1)
                    c = slice(kk * GROUP, (kk + 1) * GROUP)
                    nc.vector.tensor_tensor(dst[:, b % 2, LO, c], bank[T_BANK[kk]][:, :], dst[:, b % 2, HI, c].bitcast(F32),
                                            ALU.subtract).then_inc(done, 1)

            def rows_low(s, used, src, i, o):
                if skip(i, o, TILES):
                    return
                t, k, b = at(i, o, EB)
                dve.wait_ge(s["T_hi"], t + 1)
                freed(dve, s[used], i, o, 2)
                for dst, psum in src:
                    last = nc.vector.tensor_tensor(dst[:, b % 2, LO, :], psum, dst[:, b % 2, HI, :].bitcast(F32), ALU.subtract)
                last.then_inc(s["T_lo"], 1)

            def y_sum(i, o):
                if skip(i, o, GROUPS):
                    return
                g, k, b = at(i, o, DB)
                dve.wait_ge(y_stored[b], 16 * k)
                for m in range(2):
                    dve.wait_ge(y_psum, 2 * g + m + 1)
                    c = slice(m * 2 * D, (m + 1) * 2 * D)
                    nc.vector.tensor_tensor(d_y[:, b, c], bank[W_BANK[m]][:, :], d_x1[:, b, c], ALU.add).then_inc(y_step, 1)

            def y_stats(i, o):
                if skip(i, o, GROUPS):
                    return
                g, k, b = at(i, o, DB)
                dve.wait_ge(y_step, Y_STEPS * g + 2)
                freed(dve, factor_step[1], i, o, 2, 2)
                ch = Chain(dve, y_step, g, Y_STEPS)
                ch.j = 2
                row_stats(ch, 1, d_y, b)

            def equal(s, i, o):
                if skip(i, o, TILES):
                    return
                t, k, b = at(i, o, EB)
                arrived(dve, s, "row_in", k, b)
                freed(dve, s["tot"], i, o, EB)
                nc.vector.tensor_scalar(e_eq[:, b, :], e_row[:, b, :], dst_f[:, bass.ds(t, 1)], None, ALU.is_equal).then_inc(s["eq"], 1)

            def row_moments(ch, b):
                ch.add(nc.vector.bn_stats(e_st[:, :], e_z[:, b, :]))
                settle(dve)
                ch.add(nc.vector.bn_aggr(e_mv[:, b, :], e_st[:, :]))

            def tile_factors(s, i, o):
                if skip(i, o, TILES):
                    return
                t, k, b = at(i, o, EB)
                dve.wait_ge(s["dev"], t + 1)
                freed(dve, s["o"], i, o, EB)
                factors(Chain(dve, s["factor"], t, 2), e_rs[:, b, 0:1], e_rs[:, b, 1:2], e_mv[:, b, 0:1], e_dev[:, b:b + 1])

            def g_rows(i, o):
                if skip(i, o, TILES):
                    return
                t, k, b = at(i, o, EB)
                dve.wait_ge(G0["deg"], t + 1)
                dve.wait_ge(G0["dst_biased"], t + 1)
                freed(dve, G0["o"], i, o, EB)
                if not (isinstance(i, int) and o < 1):
                    dve.wait_ge(G0["fin"], FIN_STEPS[0] * t)
                ch = Chain(dve, G0["fin"], t, FIN_STEPS[0])
                ch.add(nc.vector.tensor_scalar(e_nrm[:, 0:1], e_sd[:, b:b + 1], 1.0, None, ALU.max))
                ch.add(nc.vector.reciprocal(e_nrm[:, 0:1], e_nrm[:, 0:1]))
                ch.add(nc.vector.scalar_tensor_tensor(e_z[:, b, :], bank[GTOT_BANK[b % 2]][:, 0:D], e_nrm[:, 0:1], e_dst[:, b, :], ALU.mult, ALU.add))
                row_moments(ch, b)

            def first_pass(i, o):
                group_factors(0, i, o + 2)
                x_stats(i, o + 3)
                group_factors(1, i, o - 2)
                low_parts(x1T_hi, x1T_lo, h_psum, d_x1T, i, o + 1)
                rows_low(G0, "M_psum", ((e_inT, bank[GT_BANK][:, :]),), i, o + 1)
                equal(G0, i, o)
                tile_factors(G0, i, o - 3)
                y_sum(i, o - 1)
                g_rows(i, o - 2)
                low_parts(hT_hi, hT_lo, y_psum, d_hT, i, o)
                y_stats(i, o - 1)
            run(dve, first_pass, GROUPS, 3, 3, TILES - GROUPS)

            for l in range(2):
                s, c, m = A[l], CB[l], SM[l]

                def attend(i, o):
                    rows_low(s, "v_psum", transposed(o + 1), i, o + 1)
                    if skip(i, o, TILES):
                        return
                    t, k, b = at(i, o, EB)
                    dve.wait_ge(s["k_psum"], t + 1)
                    dve.wait_ge(s["qs_out"], t + 1)
                    if not (isinstance(i, int) and o < 1):
                        dve.wait_ge(s["score"], 2 * t)
                    ch = Chain(dve, s["score"], t, 2)
                    ch.add(nc.vector.tensor_tensor(e_prod[:, :], bank[3 + b % 2][:, 0:D], e_qs[:, b, 0:D], ALU.mult))
                    ch.add(nc.vector.tensor_reduce(alpha[:, bass.ds(t * H, H)], e_prod[:, :].rearrange("p (h c) -> p h c", h=H), AX.X, ALU.add))
                    if l:
                        arrived(dve, s, "res_in", k, b)
                        nc.vector.tensor_tensor(e_qs[:, b, D:2 * D], e_qs[:, b, D:2 * D], e_res[:, b, :], ALU.add).then_inc(s["res_added"], 1)
                run(dve, attend, TILES, 0, 1)

                dve.wait_ge(s["score"], 2 * TILES)
                nc.vector.memset(alpha[0:1, :], -BIG).then_inc(m["masked"], 1)
                ch = Chain(dve, m["step"], 0, SM_STEPS)
                dve.wait_ge(m["aT"], 1)
                ch.add(nc.vector.tensor_copy(m_a[:, :], bank[7][0:TILES, :]))

                def scans(carried):
                    for h in range(H):
                        f = m_f[:, h * P:(h + 1) * P]
                        r = m_r[:, h * P:(h + 1) * P]
                        x = m_a[:, h * P:(h + 1) * P]
                        nc.vector.tensor_tensor_scan(f, m_same[:, 0, :], x, m_cin[:, h:h + 1] if carried else -BIG, ALU.min, ALU.max)
                        last = nc.vector.tensor_tensor_scan(r[:, ::-1], m_same[:, 1, ::-1], x[:, ::-1],
                                                            m_cin[:, 32 + h:33 + h] if carried else -BIG, ALU.min, ALU.max)
                    ch.add(last)
                scans(False)
                ch.add(nc.vector.tensor_copy(m_end[:, 0:H], m_f.rearrange("t (h s) -> t h s", h=H)[:, :, P - 1]))
                ch.add(nc.vector.tensor_copy(m_end[:, 32:32 + H], m_r.rearrange("t (h s) -> t h s", h=H)[:, :, 0]))
                dve.wait_ge(m["ends"], 1)
                ch.add(nc.vector.tensor_copy(m_rows[:, :], bank[0][0:64, 0:TILES]))
                fw, bw = slice(0, 32), slice(32, 64)
                ch.add(nc.vector.tensor_tensor_scan(m_scan[fw, :], m_gate[fw, 0, :], m_rows[fw, :], -BIG, ALU.min, ALU.max))
                ch.add(nc.vector.tensor_tensor_scan(m_scan[bw, ::-1], m_gate[bw, 0, ::-1], m_rows[bw, ::-1], -BIG, ALU.min, ALU.max))
                ch.add(nc.vector.memset(m_in[:, :], -BIG))
                ch.add(nc.vector.tensor_tensor(m_in[fw, 1:TILES], m_scan[fw, 0:TILES - 1], m_gate[fw, 1, 1:TILES], ALU.min))
                ch.add(nc.vector.tensor_tensor(m_in[bw, 0:TILES - 1], m_scan[bw, 1:TILES], m_gate[bw, 1, 0:TILES - 1], ALU.min))
                dve.wait_ge(m["cin"], 1)
                ch.add(nc.vector.tensor_copy(m_cin[:, :], bank[1][0:TILES, 0:64]))
                scans(True)
                ch.add(nc.vector.tensor_tensor(m_f[:, :], m_f[:, :], m_r[:, :], ALU.max))
                dve.wait_ge(m["max_psum"], 1)
                nc.vector.tensor_tensor(ex.rearrange("p (t h) -> p h t", h=H), alpha.rearrange("p (t h) -> p h t", h=H),
                                        bank[7][:, 0:H * TILES].rearrange("p (h t) -> p h t", h=H), ALU.subtract).then_inc(m["max"], 1)

                def combine(i, o):
                    have = not skip(i, o - 1, TILES)
                    if have:
                        t, k, b = at(i, o - 1, EB)
                        tot = bank[b]
                        dve.wait_ge(c["tot"], t + 1)
                        if not (isinstance(i, int) and o == TILES):
                            dve.wait_ge(c["carry"], t + 2)
                        arrived(dve, c, "self_in", k, b)
                        freed(dve, c["o"], i, o - 1, EB)
                        if not (isinstance(i, int) and o <= 1):
                            dve.wait_ge(c["fin"], FIN_STEPS[1 + l] * t)
                        ch = Steps(dve, c["fin"], t, FIN_STEPS[1 + l])
                        ch.start()
                        ch.end(nc.vector.tensor_scalar(e_nrm[:, 0:H], tot[:, D:CW], SOFTMAX_EPS, None, ALU.add))
                    past = l and not skip(i, o - 3, TILES)
                    if past:
                        u, ku, bu = at(i, o - 3, EB)
                        dve.wait_ge(c["dev"], u + 1)
                        freed(dve, c["o"], i, o - 3, EB)
                        cf = Steps(dve, c["factor"], u, 2)
                        cf.start()
                        cf.end(nc.vector.reciprocal(e_rs[:, bu, 0:1], e_dev[:, bu:bu + 1]))
                    if have:
                        ch.start()
                        ch.end(nc.vector.reciprocal(e_nrm[:, 0:H], e_nrm[:, 0:H]))
                    if past:
                        cf.start()
                        cf.end(nc.vector.scalar_tensor_tensor(e_rs[:, bu, 1:2], e_mv[:, bu, 0:1], -1.0, e_rs[:, bu, 0:1],
                                                              ALU.mult, ALU.mult))
                    if not l:
                        equal(c, i, o + 2)
                    if have:
                        ch.start()
                        for h in range(H):
                            col = slice(h * C, (h + 1) * C)
                            last = nc.vector.scalar_tensor_tensor(e_z[:, b, col], tot[:, col], e_nrm[:, h:h + 1],
                                                                  e_res[:, b, col], ALU.mult, ALU.add)
                        ch.end(last)
                        if l:
                            ch.start()
                            ch.end(nc.vector.bn_stats(e_st[:, :], e_z[:, b, :]))
                    if l:
                        equal(c, i, o + 2)
                    if l and have:
                        ch.start()
                        settle(dve)
                        ch.end(nc.vector.bn_aggr(e_mv[:, b, :], e_st[:, :]))
                run(dve, combine, TILES, 1 + 2 * l, 2)

        @block.tensor
        def _(pe):
            pe.wait_ge(ident_done, 2)
            pe.wait_ge(prep_done, 5)
            pe.wait_ge(weights_lo, 3)
            pe.wait_ge(bias_moved, 16 * 4)

            def transpose_group(src, done, i, o, ready, read, before, times):
                if skip(i, o, GROUPS):
                    return
                g, k, b = at(i, o, DB)
                pe.wait_ge(ready, (g + 1) * times)
                n = g - before
                if not (isinstance(i, int) and not 0 <= n < GROUPS):
                    pe.wait_ge(read, 2 * (n + 1))
                for kk in range(2):
                    for j in range(J):
                        last = nc.tensor.transpose(bank[T_BANK[kk]][:, j * P:(j + 1) * P],
                                                   src[:, b, j * D + kk * P:j * D + (kk + 1) * P], ident[:, :])
                last.then_inc(done, 1)

            def product(srcT, layer, done, i, o, parts, read, before, times):
                if skip(i, o, GROUPS):
                    return
                g, k, b = at(i, o, DB)
                pe.wait_ge(parts, 2 * (g + 1))
                n = g - before
                for m in range(2):
                    if not (isinstance(i, int) and not 0 <= n < GROUPS):
                        pe.wait_ge(read, n * times + m + 1)
                    for jj in range(2):
                        j = 2 * m + jj
                        dst = bank[W_BANK[m]][:, jj * D:(jj + 1) * D]
                        nc.tensor.matmul(dst, ones_bf[:, :], bias_mm[:, 2 * layer, D:2 * D], start=True, stop=False)
                        for d, w in PASSES:
                            for kk in range(2):
                                last = nc.tensor.matmul(dst, srcT[:, b % 2, d, kk * GROUP + j * P:kk * GROUP + (j + 1) * P],
                                                        w_qs[layer][:, w, kk, D:2 * D], start=False,
                                                        stop=(d, w, kk) == (HI, HI, 1))
                    last.then_inc(done, 1)

            def sums(s, rhs, width, tot, free, i, o):
                if skip(i, o, TILES):
                    return
                t, k, b = at(i, o, EB)
                pe.wait_ge(s["eq"], t + 1)
                pe.wait_ge(s["carry"], t + 1)
                freed(pe, s["fin"], i, o, free[0], free[1])
                nc.tensor.matmul(tot[:, 0:width], e_eq[:, b, :], rhs[:, b, 0:width], start=True, stop=True).then_inc(s["tot"], 1)

            def cols(t, b, k):
                return t[:, b, k * P:(k + 1) * P]

            def part_cols(b, part, k):
                return e_inT[:, b % 2, part, k * P:(k + 1) * P]

            def g_transposes(i, o):
                if skip(i, o, TILES):
                    return
                t, k, b = at(i, o, EB)
                arrived(pe, G0, "src_in", k, b)
                arrived(pe, G0, "attr_in", k, b)
                freed(pe, G0["T_lo"], i, o, 1)
                for kk in range(4):
                    last = nc.tensor.transpose(cols_of(bank[GT_BANK], kk), cols((e_src, e_attr)[kk // 2], b, kk % 2), ident[:, :])
                last.then_inc(G0["T_psum"], 1)

            def cols_of(t, k):
                return t[:, k * P:(k + 1) * P]

            def messages(i, o):
                if skip(i, o, TILES):
                    return
                t, k, b = at(i, o, EB)
                pe.wait_ge(G0["T_lo"], t + 1)
                freed(pe, G0["rhs_in"], i, o, 1)
                for d, w in PASSES:
                    for kk in range(4):
                        last = nc.tensor.matmul(bank[GM_BANK][:, 0:D], part_cols(b, d, kk), w0[:, w, kk, :],
                                                start=(d, w, kk) == (LO, HI, 0), stop=(d, w, kk) == (HI, HI, 3))
                last.then_inc(G0["M_psum"], 1)

            def first_pass(i, o):
                product(d_x1T, 0, h_psum, i, o, x1T_lo, y_step, 2, Y_STEPS)
                transpose_group(d_x1, x1T_psum, i, o + 1, x1_done, hT_lo, 2, 1)
                g_transposes(i, o + 1)
                product(d_hT, 1, y_psum, i, o - 1, hT_lo, h_done, -1, 2)
                transpose_group(d_h, hT_psum, i, o, h_done, x1T_lo, -1, 2)
                messages(i, o)
                sums(G0, e_rhs, D + 1, bank[GTOT_BANK[(o - 1) % 2]], (2, FIN_STEPS[0]), i, o - 1)
            run(pe, first_pass, GROUPS, 1, 1, TILES - GROUPS)

            pe.wait_ge(weights_lo, len(raw_weights))
            for l in range(2):
                s, c, m = A[l], CB[l], SM[l]

                def transposes(i, o):
                    if skip(i, o, TILES):
                        return
                    t, k, b = at(i, o, EB)
                    for n in ("src_in", "attr_in", "dst_in"):
                        arrived(pe, s, n, k, b)
                    freed(pe, s["T_lo"], i, o, 2)
                    if not (isinstance(i, int) and o < 2):
                        pe.wait_ge(s["score"], 2 * (t - 2) + 1)
                    for kk in range(4):
                        nc.tensor.transpose(cols_of(bank[o % 2], kk), cols((e_src, e_dst)[kk // 2], b, kk % 2), ident[:, :])
                    nc.tensor.transpose(bank[3 + o % 2][:, D:D + P], e_attr[:, b, 0:P], ident[:, :]).then_inc(s["T_psum"], 1)

                def attend(i, o):
                    transposes(i, o + 1)
                    if skip(i, o, TILES):
                        return
                    t, k, b = at(i, o, EB)
                    q = o % 2
                    pe.wait_ge(s["T_lo"], t + 1)
                    freed(pe, s["qs_out"], i, o, 2)

                    def project(out_, bias, w, col, attr, first):
                        width = out_.shape[-1]
                        nc.tensor.matmul(out_, ones_bf[:, :], bias, start=True, stop=False)
                        for d, p in PASSES:
                            if attr:
                                nc.tensor.matmul(out_, e_atT[:, q, d, :], w_e[l][:, p, 0, :], start=False, stop=False)
                            for kk in range(2):
                                last = nc.tensor.matmul(out_, part_cols(b, d, first + kk), w[:, p, kk, col:col + width],
                                                        start=False, stop=(d, p, kk) == (HI, HI, 1))
                        return last

                    project(bank[5 + q][:, :], bias_mm[:, 2 * l, :], w_qs[l], 0, False, 2).then_inc(s["qs_psum"], 1)
                    project(bank[3 + q][:, 0:D], bias_mm[:, 2 * l + 1, 0:D], w_kv[l], 0, True, 0).then_inc(s["k_psum"], 1)
                    freed(pe, s["v_out"], i, o, 2)
                    project(bank[(2, 7)[q]][:, 0:D], bias_mm[:, 2 * l + 1, D:2 * D], w_kv[l], D, True, 0).then_inc(s["v_psum"], 1)
                run(pe, attend, TILES, 0, 1)

                pe.wait_ge(m["masked"], 1)
                pe.wait_ge(s["v_out"], TILES)
                for h in range(H):
                    last = nc.tensor.transpose(bank[7][0:TILES, h * P:(h + 1) * P], alpha.rearrange("p (t h) -> p h t", h=H)[:, h, :], ident[:, :])
                last.then_inc(m["aT"], 1)
                pe.wait_ge(m["step"], 4)
                nc.tensor.transpose(bank[0][:, 0:TILES], m_end[:, :], ident[0:TILES, 0:TILES]).then_inc(m["ends"], 1)
                pe.wait_ge(m["step"], 10)
                nc.tensor.matmul(bank[1][0:TILES, 0:64], m_in[:, :], ident[0:64, 0:64], start=True, stop=True).then_inc(m["cin"], 1)
                pe.wait_ge(m["step"], SM_STEPS)
                for h in range(H):
                    last = nc.tensor.transpose(bank[7][:, h * TILES:(h + 1) * TILES], m_f[:, h * P:(h + 1) * P], ident[0:TILES, 0:TILES])
                last.then_inc(m["max_psum"], 1)
                run(pe, lambda i, o: sums(c, e_rhs, CW, bank[o % EB], (EB, FIN_STEPS[1 + l]), i, o), TILES, 0, 0)


SPLIT_STEPS = 2 * (1 + 2 * 5)
SM_STEPS = 13
UNROLL = 4

def layout(inputs):
    pad = N

    def rows(v, fill):
        full = np.full((TILES * EPT,) + v.shape[1:], fill, v.dtype)
        full[:E] = v
        return full.reshape((TILES, EPT) + v.shape[1:])

    def attr(v):
        slots = np.zeros((TILES, P, v.shape[1]), v.dtype)
        slots[:, 1:] = rows(v, 0)
        return slots.reshape(TILES * P, v.shape[1])

    dst = rows(np.asarray(inputs["dst"]), pad)
    src = rows(np.asarray(inputs["src"]), 0)
    none = np.full((1,), -1, dst.dtype)
    after = np.concatenate([dst.reshape(-1)[1:], none]).reshape(TILES, EPT)
    first, last = dst[:, 0], dst[:, -1]
    next_first = np.concatenate([first[1:], none])
    prev_last = np.concatenate([none, last[:-1]])
    slots = np.concatenate([first[:, None], dst], 1)
    return {
        "src_slots": np.concatenate([src[:, :1], src], 1).T,
        "dst_slots": slots.T,
        "dst_next": np.concatenate([first[:, None], after], 1).T,
        "dst_rows": np.concatenate([next_first[:, None], dst], 1),
        "dst_tiles": np.concatenate([first[:, None], slots, last[:, None]], 1),
        "tile_ends": np.stack([first, last, prev_last, next_first]),
        "attr_128": attr(np.asarray(inputs["edge_attr_128"])),
        "attr_256": attr(np.asarray(inputs["edge_attr_256"])),
    }


def kernel(**inputs):
    import concourse.bacc as bacc
    from concourse import mybir as mb
    from concourse.bass_utils import run_bass_kernel_spmd

    arrays = {n: np.asarray(v) for n, v in inputs.items() if n not in ("src", "dst", "edge_attr_128", "edge_attr_256")}
    arrays.update(layout(inputs))
    arrays = {f"in_{n}": np.ascontiguousarray(v) for n, v in arrays.items()}
    nc = bacc.Bacc("TRN2", target_bir_lowering=False, num_devices=1)
    args = {n[3:]: nc.dram_tensor(n, v.shape, mb.dt.from_np(v.dtype), kind="ExternalInput").ap() for n, v in arrays.items()}
    out = nc.dram_tensor("out", (N, D), mb.dt.float32, kind="ExternalOutput").ap()
    build(nc, args, out)
    return run_bass_kernel_spmd(nc, [arrays], core_ids=[0]).results[0]["out"]
```

```python
import numpy as np
import concourse.bass as bass
import concourse.mybir as mybir
from contextlib import ExitStack

F32 = mybir.dt.float32
F32R = mybir.dt.float32r
BF16 = mybir.dt.bfloat16
I32 = mybir.dt.int32
ALU = mybir.AluOpType
ACT = mybir.ActivationFunctionType
AX = mybir.AxisListType

P = 128
N, D, ED, H, E = 50000, 256, 128, 4, 12500
C = D // H
EPT = P - 1
EB = 4
TILES = EB * -(-E // (EB * EPT))
J = 4
GROUP = P * J
GROUPS = -(-N // GROUP)
DB = EB
UNROLL = 2 * EB
LN_EPS = 1e-5
SOFTMAX_EPS = 1e-16
BIG = float(2 ** 100)
CW = D + H
HI, LO = 0, 1
PASSES = ((LO, HI), (HI, LO), (HI, HI))


def build(nc, a, out):
    ctx = ExitStack()
    with ctx:
        def sb(name, shape, dt=F32):
            return ctx.enter_context(nc.sbuf_tensor(name, shape, dt))

        def pb(name):
            return ctx.enter_context(nc.psum_tensor(name, [P, 512], F32))

        def sem(name):
            return ctx.enter_context(nc.semaphore(name))

        def sems(name, n):
            return [sem(f"{name}{i}") for i in range(n)]

        x1_table = nc.dram_tensor("x1_table", [N, D], F32).ap()
        h_table = nc.dram_tensor("h_table", [N, D], F32).ap()
        x1_spill = nc.dram_tensor("x1_spill", [TILES, P, D], F32).ap()
        self_spill = [nc.dram_tensor(f"self_spill{l}", [TILES, P, D], F32).ap() for l in range(2)]

        ident = sb("ident", [P, P])
        ones_bf = sb("ones_bf", [P, P], BF16)
        w0 = sb("w0", [P, 2, 4, D], F32R)
        w_qs = [sb(f"w_qs{l}", [P, 2, 2, 2 * D], F32R) for l in range(2)]
        w_kv = [sb(f"w_kv{l}", [P, 2, 2, 2 * D], F32R) for l in range(2)]
        w_e = [sb(f"w_e{l}", [P, 2, 1, D], F32R) for l in range(2)]
        b0_all = sb("b0_all", [P, D])
        bias_mm = sb("bias_mm", [P, 4, 2 * D], BF16)
        src_idx = sb("src_idx", [P, TILES], I32)
        dst_idx = sb("dst_idx", [P, TILES], I32)
        dst_next = sb("dst_next", [P, TILES], I32)
        dst_f = sb("dst_f", [P, TILES])
        last_idx = sb("last_idx", [P, TILES], I32)
        alpha = sb("alpha", [P, TILES * H])
        ex = sb("ex", [P, TILES * H])

        GD = J * D
        with ExitStack() as dense_space:
            def dense_buf(name, shape, dt=F32):
                return dense_space.enter_context(nc.sbuf_tensor(name, [P] + shape, dt))
            d_x, d_x1, d_h, d_y = (dense_buf(n, [DB, GD]) for n in ("d_x", "d_x1", "d_h", "d_y"))
            d_x1T, d_hT = (dense_buf(n, [2, 2, GD], F32R) for n in ("d_x1T", "d_hT"))
        assert (4 * DB + 2 * 4) * GD <= TILES * D
        vals = sb("vals", [P, TILES * D])

        def early(t, lo, shape, names, **sizes):
            n = int(np.prod(shape))
            return t.rearrange("p b n -> p (b n)")[:, lo:lo + n].rearrange(f"p ({names}) -> p {names}", **sizes)
        bias_row = early(d_h, 0, (1, 2 * D), "r n", r=1)[0:4, 0]
        be_row = early(d_h, 2 * D, (1, 2 * D), "r n", r=1)[0:4, 0]
        bias_hi = d_y.rearrange("p b n -> p (b n)")[0:4, 0:3 * D].bitcast(BF16).rearrange(
            "i (r n) -> i r n", r=3)
        raw_weights = [(w_qs[0], D, "L1_gnn_Ws1", early(d_h, 12 * D, (2, D), "k n", k=2)),
                       (w_qs[1], D, "L1_gnn_Ws2", early(d_h, 14 * D, (2, D), "k n", k=2)),
                       (w0, 0, "L0_gnn_weights", early(d_y, 12 * D, (4, D), "k n", k=4))]
        at_column = 0
        for l in range(2):
            for t, col, n, chunks in ((w_qs[l], 0, "Wq", 2), (w_kv[l], 0, "Wk", 2), (w_kv[l], D, "Wv", 2), (w_e[l], 0, "We", 1)):
                raw_weights.append((t, col, f"L1_gnn_{n}{l + 1}", early(d_x1, at_column, (chunks, D), "k n", k=chunks)))
                at_column += chunks * D

        d_st = sb("d_st", [P, 2, J, 6])
        d_mv = sb("d_mv", [P, 2, 2, J, 2])
        d_dev = sb("d_dev", [P, 2, J])
        d_rs = sb("d_rs", [P, 2, 2, J])

        e_src = sb("e_src", [P, EB, D])
        e_dst = sb("e_dst", [P, EB, D])
        e_res = sb("e_res", [P, EB, D])
        e_attr = sb("e_attr", [P, EB, D])
        e_inT = sb("e_inT", [P, 2, 2, 4 * P], F32R)
        e_atT = sb("e_atT", [P, 2, 2, P], F32R)
        zero_row = sb("zero_row", [1, CW])
        ln_eps = sb("ln_eps", [P, 1])
        e_rhs = sb("e_rhs", [P, EB, CW])
        e_edge = e_rhs[:, :, 0:D]
        e_row = sb("e_row", [P, EB, P], I32)
        e_eq = sb("e_eq", [P, EB, P])
        e_prod = sb("e_prod", [P, D])
        e_zo = sb("e_zo", [P, 2, EB, D])
        e_z, e_o = e_zo[:, 0], e_zo[:, 1]
        e_qs = e_zo.rearrange("p r b d -> p (r b d)").rearrange("p (b n) -> p b n", b=EB)
        e_st = sb("e_st", [P, 6])
        e_mv = sb("e_mv", [P, EB, 2])
        e_sd = sb("e_sd", [P, EB])
        e_dev = sb("e_dev", [P, EB])
        e_rs = sb("e_rs", [P, EB, 2])
        e_nrm = sb("e_nrm", [P, 4])
        e_sx = [sb(f"e_sx{i}", [P, 1], I32) for i in range(EB)]
        e_rx = [sb(f"e_rx{i}", [P, 1], I32) for i in range(EB)]
        e_dx = [sb(f"e_dx{i}", [P, 1], I32) for i in range(EB)]
        e_lx = [sb(f"e_lx{i}", [P, 1], I32) for i in range(EB)]

        m_dst = sb("m_dst", [TILES, P + 2], I32)
        m_same = sb("m_same", [TILES, 2, P])
        m_a, m_f = (e_src.rearrange("p b d -> p (b d)")[0:TILES, i * H * P:(i + 1) * H * P] for i in range(2))
        m_r = e_attr.rearrange("p b d -> p (b d)")[0:TILES, 0:H * P]
        m_end = sb("m_end", [TILES, P])
        m_edge = sb("m_edge", [64, 4, TILES], I32)
        m_gate = sb("m_gate", [64, 2, TILES])
        m_rows = sb("m_rows", [64, TILES])
        m_scan = sb("m_scan", [64, TILES])
        m_in = sb("m_in", [64, TILES])
        m_cin = sb("m_cin", [TILES, 64])

        bank = [pb(f"bank{i}") for i in range(8)]
        T_BANK, W_BANK = (0, 1), (2, 3)
        GT_BANK, GM_BANK, GTOT_BANK = 4, 5, (6, 7)

        weight_in = [sem(f"weight_in{i}") for i in range(4)]
        weights_hi = sem("weights_hi")
        weights_lo = sem("weights_lo")
        biases_in = sem("biases_in")
        b0_in = sem("b0_in")
        index_in = sem("index_in")
        ends_in = sem("ends_in")
        ident_done = sem("ident_done")
        pads_done = sem("pads_done")
        prep_done = sem("prep_done")
        split_step = sem("split_step")
        bias_moved = sem("bias_moved")

        x_loaded = sems("x_loaded", DB)
        x1_stored = sems("x1_stored", DB)
        h_stored = sems("h_stored", DB)
        y_stored = sems("y_stored", DB)
        x_biased = sem("x_biased")
        x_step = sem("x_step")
        y_step = sem("y_step")
        dev_done = sems("dev_done", 2)
        factor_step = sems("factor_step", 2)
        x1_done = sem("x1_done")
        x1T_psum = sem("x1T_psum")
        x1T_hi = sem("x1T_hi")
        x1T_lo = sem("x1T_lo")
        h_psum = sem("h_psum")
        h_done = sem("h_done")
        hT_psum = sem("hT_psum")
        hT_hi = sem("hT_hi")
        hT_lo = sem("hT_lo")
        y_psum = sem("y_psum")
        y_done = sem("y_done")

        slot = {n: sems(n, EB) for n in ("src_in", "dst_in", "attr_in", "row_in", "res_in", "self_in", "spilled", "scattered")}
        USES = TILES // EB

        def edge_sems(ph, counts, **before):
            d = {n: sem(f"{ph}_{n}") for n in counts}
            d["before"] = {n: passes * USES for n, passes in before.items()}
            return d
        G0 = edge_sems("g", ("src_in_ix", "dst_in_ix", "dst_biased", "T_psum", "T_hi", "T_lo", "M_psum", "rhs_in", "carry", "eq", "tot", "deg",
                             "fin", "dev", "factor", "o"), src_in=0, dst_in=0, attr_in=0, row_in=0, spilled=0)
        R0 = edge_sems("r", ("scattered_ix",), self_in=0, row_in=1, scattered=0)
        A = [edge_sems(f"a{l}", ("src_in_ix", "dst_in_ix", "T_psum", "T_hi", "T_lo", "qs_psum", "v_psum", "e_out",
                                 "qs_out", "v_out", "score") + (("res_in_ix", "res_added") if l else ()),
                       src_in=1 + l, dst_in=1 + l, attr_in=1 + l, res_in=0, spilled=1 + l) for l in range(2)]
        CB = [edge_sems(f"c{l}", ("scattered_ix", "weighed", "carry", "eq", "tot", "fin", "o") + (("dev", "factor") if l else ()),
                        row_in=1 + l, self_in=l, scattered=1 + l) for l in range(2)]
        for c in CB:
            c["before"]["self_in"] += len(range(0, TILES, 2 * EB))
            c["before"]["row_in"] += len(range(EB, TILES, 2 * EB))
        SM = [edge_sems(f"s{l}", ("masked", "aT", "step", "ends", "cin", "max_psum", "max", "exp")) for l in range(2)]
        settled = sem("settled")
        m_step = sem("m_step")
        idx_step = sem("idx_step")

        def at(i, o, n):
            return n * i + o, i + o // n, o % n

        def settle(eng):
            eng.sem_inc(settled)

        def skip(i, o, total):
            return isinstance(i, int) and not 0 <= o < total

        def freed(eng, s, i, o, n, times=1):
            if isinstance(i, int) and o < n:
                return
            eng.wait_ge(s, (EB * i + o - n + 1) * times)

        def arrived(eng, s, what, k, b):
            eng.wait_ge(slot[what][b], 16 * (k + s["before"][what] + 1))

        def over(eng, s, what, k, b):
            eng.wait_ge(slot[what][b], 16 * (k + s["before"][what]))

        def redo_buffer(o):
            return (e_res, "self_in") if o % (2 * EB) < EB else (e_dst, "row_in")

        def all_over(eng, s, what):
            for b in range(EB):
                eng.wait_ge(slot[what][b], 16 * (s["before"][what] + USES))

        def run(eng, f, total, back, ahead, more=0):
            start = back + EB
            rounds = (total - ahead - start) // UNROLL
            step = UNROLL // EB
            for o in range(-ahead, start):
                f(0, o)
            with eng.Fori(0, (rounds - 1) * step + 1, step) as i:
                for o in range(start, start + UNROLL):
                    f(i, o)
            for o in range(start + rounds * UNROLL, total + more + back):
                f(0, o)

        class Chain:
            def __init__(self, eng, s, item, steps):
                self.eng, self.s, self.base, self.steps, self.j = eng, s, item * steps, steps, 0

            def add(self, ins):
                self.j += 1
                ins.then_inc(self.s, 1)
                if self.j < self.steps:
                    self.eng.wait_ge(self.s, self.base + self.j)

        def transposed(o):
            return (e_inT, bank[o % 2][:, :]), (e_atT, bank[3 + o % 2][:, D:D + P])

        class Steps(Chain):
            def start(self):
                if self.j:
                    self.eng.wait_ge(self.s, self.base + self.j)

            def end(self, ins):
                self.j += 1
                ins.then_inc(self.s, 1)

        X_STEPS, Y_STEPS = 2, 4
        SCORE_STEPS = 3
        FIN_STEPS = (5, 3, 5)

        def dense_base(i, o):
            return N - GROUP if isinstance(i, int) and o == GROUPS - 1 else GROUP * (DB * i + o)

        def node_rows(t, base, lo=0):
            return t[bass.ds(base + lo * J, (P - lo) * J), :].rearrange("(p j) d -> p (j d)", j=J)

        def tile_of(t, n):
            return t[bass.ds(n, 1), :, :].rearrange("o p d -> (o p) d")

        def all_uses(b, total):
            return 16 * len(range(b, total, DB))

        block = ctx.enter_context(nc.Block())

        @block.sync
        def _(sp):
            sp.dma_start(b0_all[:, :], a["L0_gnn_h_bias"].rearrange("(o n) -> o n", o=1).to_broadcast([P, D])).then_inc(b0_in, 16)

            def load_x(i, o):
                if skip(i, o, GROUPS):
                    return
                g, k, b = at(i, o, DB)
                freed(sp, x1_done, i, o, DB)
                sp.dma_start(d_x[:, b, :], node_rows(a["x"], dense_base(i, o))).then_inc(x_loaded[b], 16)
            for o in range(2):
                load_x(0, o)
            for t, s in ((src_idx, "src_slots"), (dst_idx, "dst_slots"), (dst_next, "dst_next")):
                sp.dma_start(t[:, :], a[s]).then_inc(index_in, 16)
            def load_weight(n):
                t, col, name, raw = raw_weights[n]
                sp.dma_start(raw, a[name].rearrange("(k p) n -> p k n", p=P)).then_inc(weight_in[min(n, 3)], 16)
            for n in range(2):
                load_weight(n)
            sp.wait_ge(split_step, 1)
            for l in range(2):
                for r, t, b, o in ((0, bias_row, "bq", 0), (0, bias_row, "bs", D), (1, bias_row, "bk", 0),
                                   (1, bias_row, "bv", D), (1, be_row, "be", 0), (1, be_row, "be", D)):
                    sp.dma_start(t[2 * l + r:2 * l + r + 1, o:o + D],
                                 a[f"L1_gnn_{b}{l + 1}"].rearrange("(o n) -> o n", o=1)).then_inc(biases_in, 16)
            for n in range(2, len(raw_weights)):
                load_weight(n)
            sp.dma_start(m_dst[:, :], a["dst_tiles"]).then_inc(ends_in, 16)
            for r in range(4):
                sp.dma_start(m_edge[:, r, :], a["tile_ends"][r:r + 1, :].to_broadcast([64, TILES])).then_inc(ends_in, 16)
            for o in range(2, 4):
                load_x(0, o)
            sp.wait_ge(split_step, SPLIT_STEPS)
            sp.wait_ge(prep_done, 1)
            for i in range(4):
                sp.dma_start(bias_mm[0:3, i, :], bias_hi[i:i + 1, :, :]).then_inc(bias_moved, 16)

            def store(i, o, src, table, done, stored, times=1):
                if skip(i, o, GROUPS):
                    return
                g, k, b = at(i, o, DB)
                sp.wait_ge(done, (g + 1) * times)
                lo = (GROUPS * GROUP - N) // J if isinstance(i, int) and o == GROUPS - 1 else 0
                sp.dma_start(node_rows(table, dense_base(i, o), lo), src[lo:, b, :]).then_inc(stored[b], 16)

            def load_row(s, i, o):
                if skip(i, o, TILES):
                    return
                t, k, b = at(i, o, EB)
                freed(sp, s["eq"], i, o, EB)
                settle(sp)
                sp.dma_start(e_row[:, b, :], a["dst_rows"][bass.ds(t, 1), :].to_broadcast([P, P])).then_inc(slot["row_in"][b], 16)

            def load_attr(s, attr, width, i, o):
                if skip(i, o, TILES):
                    return
                t, k, b = at(i, o, EB)
                freed(sp, s["T_psum"], i, o, EB)
                sp.dma_start(e_attr[:, b, 0:width], attr[bass.ds(t * P, P), :]).then_inc(slot["attr_in"][b], 16)

            def spill(s, done, src, table, i, o):
                if skip(i, o, TILES):
                    return
                t, k, b = at(i, o, EB)
                sp.wait_ge(done, t + 1)
                sp.dma_start(tile_of(table, t), src(b)).then_inc(slot["spilled"][b], 16)

            def first_pass(i, o):
                load_attr(G0, a["attr_256"], 2 * ED, i, o + 3)
                load_row(G0, i, o + 2)
                if not (isinstance(i, int) and o + 5 < 4):
                    load_x(i, o + 5)
                store(i, o, d_h, h_table, h_done, h_stored, 2)
                store(i, o + 2, d_x1, x1_table, x1_done, x1_stored)
                store(i, o - 2, d_y, out, y_done, y_stored)
                spill(G0, G0["o"], lambda b: e_o[:, b, :], x1_spill, i, o - 3)
            run(sp, first_pass, GROUPS, 3, 5, TILES - GROUPS)

            all_over(sp, G0, "spilled")

            def reload(i, o):
                if skip(i, o, TILES):
                    return
                t, k, b = at(i, o, EB)
                if not (isinstance(i, int) and o < 2 * EB):
                    sp.wait_ge(slot["scattered"][b], 16 * (k - 1))
                rows, what = redo_buffer(o)
                sp.dma_start(rows[:, b, :], tile_of(x1_spill, t)).then_inc(slot[what][b], 16)
            run(sp, reload, TILES, EB, 0)

            sp.wait_ge(G0["T_psum"], TILES)
            for l in range(2):
                def attend(i, o):
                    load_attr(A[l], a["attr_128"], ED, i, o + 3)
                    spill(A[l], A[l]["res_added" if l else "qs_out"], lambda b: e_qs[:, b, D:2 * D], self_spill[l], i, o)
                run(sp, attend, TILES, 0, 3)
                all_over(sp, A[l], "spilled")

                def combine(i, o):
                    t, k, b = at(i, o, EB)
                    load_row(CB[l], i, o)
                    freed(sp, CB[l]["fin"], i, o, EB, FIN_STEPS[1 + l])
                    sp.dma_start(e_res[:, b, :], tile_of(self_spill[l], t)).then_inc(slot["self_in"][b], 16)
                if l == 0:
                    all_over(sp, R0, "scattered")
                run(sp, combine, TILES, 0, 0)

        @block.gpsimd
        def _(pool):
            nc.gpsimd.memset(ident[:, :], 0.0).then_inc(ident_done, 1)
            pool.wait_ge(ident_done, 1)
            nc.gpsimd.affine_select(out=ident[:, :], in_=ident[:, :], compare_op=ALU.not_equal, fill=1.0,
                                    base=0, pattern=[[-1, P]], channel_multiplier=1).then_inc(ident_done, 1)
            for t in (e_src, e_dst):
                nc.gpsimd.memset(t[:, :, :], 0.0).then_inc(pads_done, 1)
            pool.wait_ge(b0_in, 16)

            def bias(i, o):
                if skip(i, o, GROUPS):
                    return
                g, k, b = at(i, o, DB)
                pool.wait_ge(x_loaded[b], 16 * k + 16)
                v = d_x[:, b, :].rearrange("p (j d) -> p j d", j=J)
                nc.gpsimd.tensor_tensor(v, v, b0_all[:, None, :].to_broadcast([P, J, D]), ALU.add).then_inc(x_biased, 1)

            def number(s, what, index, ix, i, o):
                if skip(i, o, TILES):
                    return
                t, k, b = at(i, o, EB)
                over(pool, s, what, k, b)
                settle(pool)
                nc.gpsimd.tensor_copy(ix[b][:, :], index[:, bass.ds(t, 1)]).then_inc(s[what + "_ix"], 1)

            def gather(s, what, buf, table, index, ix, free, i, o):
                number(s, what, index, ix, i, o + 1)
                if skip(i, o, TILES):
                    return
                t, k, b = at(i, o, EB)
                freed(pool, free[0], i, o, EB, free[1])
                pool.wait_ge(s[what + "_ix"], t + 1)
                settle(pool)
                nc.gpsimd.indirect_dma_start(out=buf[:, b, :], out_offset=None, in_=table,
                                             in_offset=bass.IndirectOffsetOnAxis(ap=ix[b][:, :], axis=0),
                                             bounds_check=N - 1, oob_is_err=False).then_inc(slot[what][b], 16)

            def scatter(s, table, rows, ready, i, o):
                number(s, "scattered", last_idx, e_lx, i, o + 1)
                if skip(i, o, TILES):
                    return
                t, k, b = at(i, o, EB)
                pool.wait_ge(s["scattered_ix"], t + 1)
                ready(t, k, b)
                settle(pool)
                nc.gpsimd.indirect_dma_start(out=table, out_offset=bass.IndirectOffsetOnAxis(ap=e_lx[b][:, :], axis=0),
                                             in_=rows[:, b, :], in_offset=None,
                                             bounds_check=N - 1, oob_is_err=False).then_inc(slot["scattered"][b], 16)

            def bias_dst(i, o):
                if skip(i, o, TILES):
                    return
                t, k, b = at(i, o, EB)
                arrived(pool, G0, "dst_in", k, b)
                nc.gpsimd.tensor_tensor(e_dst[:, b, :], e_dst[:, b, :], b0_all[:, :], ALU.add).then_inc(G0["dst_biased"], 1)

            def first_pass(i, o):
                if isinstance(i, int) and o == -4:
                    pool.wait_ge(pads_done, 2)
                    pool.wait_ge(index_in, 48)
                    pool.wait_ge(idx_step, 3)
                bias(i, o + 4)
                bias_dst(i, o - 1)
                gather(G0, "src_in", e_src, a["x"], src_idx, e_sx, (G0["T_psum"], 1), i, o + 3)
                gather(G0, "dst_in", e_dst, a["x"], dst_idx, e_dx, (G0["fin"], FIN_STEPS[0]), i, o + 1)
            run(pool, first_pass, GROUPS, 1, 4, TILES - GROUPS)

            for b in range(DB):
                for stored in (x1_stored, h_stored, y_stored):
                    pool.wait_ge(stored[b], all_uses(b, GROUPS))
            def redo(i, o):
                rows, what = redo_buffer(o)

                def reloaded(t, k, b):
                    pool.wait_ge(slot[what][b], 8 * i + 16 * (R0["before"][what] + o // (2 * EB) + 1))
                scatter(R0, x1_table, rows, reloaded, i, o)
            run(pool, redo, TILES, EB, 1)
            all_over(pool, R0, "scattered")
            for l in range(2):
                table, residual = ((x1_table, None), (h_table, x1_table))[l]

                def attend(i, o):
                    gather(A[l], "src_in", e_src, table, src_idx, e_sx, (A[l]["T_psum"], 1), i, o)
                    gather(A[l], "dst_in", e_dst, table, dst_idx, e_dx, (A[l]["T_psum"], 1), i, o)
                    if residual is not None:
                        gather(A[l], "res_in", e_res, residual, dst_idx, e_rx, (A[l]["res_added"], 1), i, o - 2)
                run(pool, attend, TILES, 2 * l, 1)
                pool.wait_ge(SM[l]["exp"], 1)

                def weigh(i, o):
                    if skip(i, o, TILES):
                        return
                    t, k, b = at(i, o, EB)
                    freed(pool, CB[l]["tot"], i, o, EB)
                    w = ex[:, bass.ds(t * H, H)]
                    settle(pool)
                    nc.gpsimd.tensor_copy(e_rhs[:, b, D:CW], w)
                    nc.gpsimd.tensor_tensor(e_rhs[:, b, 0:D].rearrange("p (h c) -> p h c", h=H),
                                            vals[:, bass.ds(t * D, D)].rearrange("p (h c) -> p h c", h=H),
                                            w.rearrange("p (h o) -> p h o", o=1).to_broadcast([P, H, C]),
                                            ALU.mult).then_inc(CB[l]["weighed"], 1)

                def combine(i, o):
                    weigh(i, o + 3)
                    scatter(CB[l], out if l else h_table, e_o, lambda t, k, b: pool.wait_ge(CB[l]["o"], t + 1), i, o - 3 - 2 * l)
                run(pool, combine, TILES, 3 + 2 * l, 3)
                all_over(pool, CB[l], "scattered")

        @block.scalar
        def _(act):
            def norm_rows(which, i, o):
                if skip(i, o, GROUPS):
                    return
                g, k, b = at(i, o, DB)
                act.wait_ge(factor_step[which], 2 * g + 2)
                if which == 0:
                    act.wait_ge(x1_stored[b], 16 * k)
                    freed(act, y_step, i, o, DB, Y_STEPS)
                src, dst = (d_x, d_x1) if which == 0 else (d_y, d_y)
                for j in range(J):
                    last = nc.scalar.activation(dst[:, b, j * D:(j + 1) * D], src[:, b, j * D:(j + 1) * D], ACT.Identity,
                                                bias=d_rs[:, which, 1, j:j + 1], scale=d_rs[:, which, 0, j:j + 1])
                last.then_inc((x1_done, y_done)[which], 1)

            def deviations(which, i, o):
                if skip(i, o, GROUPS):
                    return
                g = at(i, o, DB)[0]
                steps = (X_STEPS, Y_STEPS)[which]
                act.wait_ge((x_step, y_step)[which], steps * (g + 1))
                if not (isinstance(i, int) and o < 1):
                    act.wait_ge(factor_step[which], 2 * g)
                nc.scalar.activation(d_dev[:, which, :], d_mv[:, which, o % 2, :, 1], ACT.Sqrt, bias=ln_eps[:, 0:1]).then_inc(dev_done[which], 1)

            def relu_h(i, o):
                if skip(i, o, GROUPS):
                    return
                g, k, b = at(i, o, DB)
                act.wait_ge(h_stored[b], 16 * k)
                for m in range(2):
                    act.wait_ge(h_psum, 2 * g + m + 1)
                    nc.scalar.activation(d_h[:, b, m * 2 * D:(m + 1) * 2 * D], bank[W_BANK[m]][:, :], ACT.Relu).then_inc(h_done, 1)

            def high_parts(psum, done, used, dst, i, o):
                if skip(i, o, GROUPS):
                    return
                g, k, b = at(i, o, DB)
                act.wait_ge(psum, g + 1)
                freed(act, used, i, o, 2, 2)
                for kk in range(2):
                    nc.scalar.activation(dst[:, b % 2, HI, kk * GROUP:(kk + 1) * GROUP], bank[T_BANK[kk]][:, :], ACT.Copy).then_inc(done, 1)

            def rows_high(s, used, src, i, o):
                if skip(i, o, TILES):
                    return
                t, k, b = at(i, o, EB)
                act.wait_ge(s["T_psum"], t + 1)
                freed(act, s[used], i, o, 2)
                for dst, psum in src:
                    nc.scalar.activation(dst[:, b % 2, HI, :], psum, ACT.Copy).then_inc(s["T_hi"], 1)

            def carry(s, below, rhs, width, tot, i, o):
                t, k, b = at(i, o, EB)
                act.wait_ge(below, t + 1)
                if isinstance(i, int) and o == 0:
                    src = zero_row[0:1, 0:width]
                else:
                    act.wait_ge(s["tot"], t)
                    src = tot[0:1, 0:width]
                nc.scalar.activation(rhs[0:1, b, 0:width], src, ACT.Copy).then_inc(s["carry"], 1)

            def deviation(s, steps, i, o):
                if skip(i, o, TILES):
                    return
                t, k, b = at(i, o, EB)
                act.wait_ge(s["fin"], steps * (t + 1))
                freed(act, s["factor"], i, o, EB, 2)
                nc.scalar.activation(e_dev[:, b:b + 1], e_mv[:, b, 1:2], ACT.Sqrt, bias=ln_eps[:, 0:1]).then_inc(s["dev"], 1)

            def finish(s, what, relu, i, o):
                if skip(i, o, TILES):
                    return
                t, k, b = at(i, o, EB)
                if relu:
                    act.wait_ge(s["fin"], FIN_STEPS[1] * (t + 1))
                else:
                    act.wait_ge(s["factor"], 2 * (t + 1))
                over(act, s, what, k, b)
                if relu:
                    nc.scalar.activation(e_o[:, b, :], e_z[:, b, :], ACT.Relu).then_inc(s["o"], 1)
                else:
                    nc.scalar.activation(e_o[:, b, :], e_z[:, b, :], ACT.Identity,
                                         bias=e_rs[:, b, 1:2], scale=e_rs[:, b, 0:1]).then_inc(s["o"], 1)

            def g_operand(i, o):
                if skip(i, o, TILES):
                    return
                t, k, b = at(i, o, EB)
                act.wait_ge(G0["M_psum"], t + 1)
                freed(act, G0["tot"], i, o, EB)
                nc.scalar.activation(e_rhs[:, b, 0:D], bank[GM_BANK][:, 0:D], ACT.Copy).then_inc(G0["rhs_in"], 1)
                carry(G0, G0["rhs_in"], e_rhs, D + 1, bank[GTOT_BANK[(b + 1) % 2]], i, o)

            def g_degree(i, o):
                if skip(i, o, TILES):
                    return
                t, k, b = at(i, o, EB)
                act.wait_ge(G0["tot"], t + 1)
                freed(act, G0["fin"], i, o, EB, FIN_STEPS[0])
                nc.scalar.activation(e_sd[:, b:b + 1], bank[GTOT_BANK[b % 2]][:, D:D + 1], ACT.Sqrt).then_inc(G0["deg"], 1)

            def first_pass(i, o):
                g_operand(i, o - 1)
                g_degree(i, o - 2)
                deviations(0, i, o + 2)
                relu_h(i, o)
                deviations(1, i, o - 2)
                high_parts(x1T_psum, x1T_hi, h_psum, d_x1T, i, o + 1)
                rows_high(G0, "M_psum", ((e_inT, bank[GT_BANK][:, :]),), i, o + 1)
                deviation(G0, FIN_STEPS[0], i, o - 3)
                norm_rows(0, i, o + 2)
                high_parts(hT_psum, hT_hi, y_psum, d_hT, i, o)
                norm_rows(1, i, o - 2)
                finish(G0, "spilled", False, i, o - 3)
            for n, (t, col, name, raw) in enumerate(raw_weights):
                act.wait_ge(weight_in[min(n, 3)], 16 if n < 3 else 16 * (len(raw_weights) - 3))
                nc.scalar.activation(t[:, HI, :, col:col + D], raw, ACT.Copy).then_inc(weights_hi, 1)
            act.wait_ge(weights_lo, len(raw_weights))
            act.wait_ge(prep_done, 5)
            run(act, first_pass, GROUPS, 3, 2, TILES - GROUPS)

            for l in range(2):
                s, c = A[l], CB[l]

                def attend(i, o):
                    if skip(i, o, TILES):
                        rows_high(s, "v_psum", transposed(o + 1), i, o + 1)
                        return
                    t, k, b = at(i, o, EB)
                    act.wait_ge(s["qs_psum"], t + 1)
                    freed(act, s["score"], i, o, EB, SCORE_STEPS)
                    over(act, s, "spilled", k, b)
                    nc.scalar.activation(e_qs[:, b, :], bank[5 + b % 2][:, :], ACT.Copy).then_inc(s["qs_out"], 1)
                    rows_high(s, "v_psum", transposed(o + 1), i, o + 1)
                    act.wait_ge(s["v_psum"], t + 1)
                    freed(act, s["v_out"], i, o, EB)
                    nc.scalar.activation(e_edge[:, b, :], bank[(2, 7)[b % 2]][:, D:2 * D], ACT.Copy).then_inc(s["e_out"], 1)
                run(act, attend, TILES, 0, 1)

                act.wait_ge(SM[l]["max"], 1)
                nc.scalar.activation(ex[:, :], ex[:, :], ACT.Exp, scale=float(C) ** -0.5).then_inc(SM[l]["exp"], 1)

                def combine(i, o):
                    if not skip(i, o, TILES):
                        carry(c, c["weighed"], e_rhs, CW, bank[(o - 1) % EB], i, o)
                    if l:
                        deviation(c, FIN_STEPS[2], i, o - 3)
                    finish(c, "scattered", l == 0, i, o - 2 - 2 * l)
                run(act, combine, TILES, 2 + 2 * l, 0)

        @block.vector
        def _(dve):
            nc.vector.memset(bias_mm[:, :, :], 0.0).then_inc(prep_done, 1)
            nc.vector.memset(zero_row[:, :], 0.0).then_inc(prep_done, 1)
            nc.vector.memset(ln_eps[:, :], LN_EPS).then_inc(prep_done, 1)
            nc.vector.memset(e_rhs[:, :, :], 1.0).then_inc(prep_done, 1)
            nc.vector.memset(ones_bf[:, :], 1.0).then_inc(prep_done, 1)

            ch = Chain(dve, split_step, 0, SPLIT_STEPS)
            ch.add(nc.vector.memset(be_row, 0.0))
            dve.wait_ge(index_in, 48)
            ix = Chain(dve, idx_step, 0, 3)
            ix.add(nc.vector.tensor_copy(dst_f[:, :], dst_idx[:, :]))
            ix.add(nc.vector.tensor_tensor(last_idx[:, :], dst_next[:, :], dst_idx[:, :], ALU.is_equal))
            ix.add(nc.vector.scalar_tensor_tensor(last_idx[:, :], last_idx[:, :], float(N), dst_idx[:, :], ALU.mult, ALU.add))

            dve.wait_ge(biases_in, 16 * 12)
            ch.add(nc.vector.tensor_tensor(bias_row, bias_row, be_row, ALU.add))
            for part in range(3):
                ch.add(nc.vector.tensor_copy(bias_hi[:, part, :], bias_row))
                if part < 2:
                    ch.add(nc.vector.tensor_tensor(bias_row, bias_row, bias_hi[:, part, :], ALU.subtract))

            for n, (t, col, name, raw) in enumerate(raw_weights):
                dve.wait_ge(weights_hi, n + 1)
                nc.vector.tensor_tensor(t[:, LO, :, col:col + D], raw, t[:, HI, :, col:col + D].bitcast(F32),
                                        ALU.subtract).then_inc(weights_lo, 1)

            def group_scale(which, i, o):
                if skip(i, o, GROUPS):
                    return
                g = at(i, o, DB)[0]
                dve.wait_ge(dev_done[which], g + 1)
                if not (isinstance(i, int) and o < 1):
                    dve.wait_ge((x1_done, y_done)[which], g)
                nc.vector.reciprocal(d_rs[:, which, 0, :], d_dev[:, which, :]).then_inc(factor_step[which], 1)

            def group_bias(which, i, o):
                if skip(i, o, GROUPS):
                    return
                g = at(i, o, DB)[0]
                dve.wait_ge(factor_step[which], 2 * g + 1)
                nc.vector.scalar_tensor_tensor(d_rs[:, which, 1, :], d_mv[:, which, o % 2, :, 0], -1.0, d_rs[:, which, 0, :],
                                               ALU.mult, ALU.mult).then_inc(factor_step[which], 1)

            def group_moments(which, i, o):
                if skip(i, o, GROUPS):
                    return
                g, k, b = at(i, o, DB)
                if which == 0:
                    dve.wait_ge(x_biased, g + 1)
                    if not (isinstance(i, int) and o < 1):
                        dve.wait_ge(x_step, X_STEPS * g)
                else:
                    dve.wait_ge(y_step, Y_STEPS * g + 2)
                for j in range(J):
                    last = nc.vector.bn_stats(d_st[:, which, j, :], (d_x, d_y)[which][:, b, j * D:(j + 1) * D])
                last.then_inc((x_step, y_step)[which], 1)

            def group_variances(which, i, o):
                if skip(i, o, GROUPS):
                    return
                g, k, b = at(i, o, DB)
                freed(dve, factor_step[which], i, o, 2, 2)
                dve.wait_ge((x_step, y_step)[which], (X_STEPS, Y_STEPS)[which] * (g + 1) - 1)
                settle(dve)
                for j in range(J):
                    last = nc.vector.bn_aggr(d_mv[:, which, b % 2, j, :], d_st[:, which, j, :])
                last.then_inc((x_step, y_step)[which], 1)

            def low_parts(psum_hi, done, used, dst, i, o):
                if skip(i, o, GROUPS):
                    return
                g, k, b = at(i, o, DB)
                freed(dve, used, i, o, 2, 2)
                for kk in range(2):
                    dve.wait_ge(psum_hi, 2 * g + kk + 1)
                    c = slice(kk * GROUP, (kk + 1) * GROUP)
                    nc.vector.tensor_tensor(dst[:, b % 2, LO, c], bank[T_BANK[kk]][:, :], dst[:, b % 2, HI, c].bitcast(F32),
                                            ALU.subtract).then_inc(done, 1)

            def rows_low(s, used, src, i, o):
                if skip(i, o, TILES):
                    return
                t, k, b = at(i, o, EB)
                freed(dve, s[used], i, o, 2)
                for n, (dst, psum) in enumerate(src):
                    dve.wait_ge(s["T_hi"], len(src) * t + n + 1)
                    last = nc.vector.tensor_tensor(dst[:, b % 2, LO, :], psum, dst[:, b % 2, HI, :].bitcast(F32), ALU.subtract)
                last.then_inc(s["T_lo"], 1)

            def y_sum(i, o):
                if skip(i, o, GROUPS):
                    return
                g, k, b = at(i, o, DB)
                dve.wait_ge(y_stored[b], 16 * k)
                for m in range(2):
                    dve.wait_ge(y_psum, 2 * g + m + 1)
                    c = slice(m * 2 * D, (m + 1) * 2 * D)
                    nc.vector.tensor_tensor(d_y[:, b, c], bank[W_BANK[m]][:, :], d_x1[:, b, c], ALU.add).then_inc(y_step, 1)

            def equal(s, i, o):
                if skip(i, o, TILES):
                    return
                t, k, b = at(i, o, EB)
                arrived(dve, s, "row_in", k, b)
                freed(dve, s["tot"], i, o, EB)
                nc.vector.tensor_scalar(e_eq[:, b, :], e_row[:, b, :], dst_f[:, bass.ds(t, 1)], None, ALU.is_equal).then_inc(s["eq"], 1)

            def tile_scale(s, i, o):
                if skip(i, o, TILES):
                    return
                t, k, b = at(i, o, EB)
                dve.wait_ge(s["dev"], t + 1)
                freed(dve, s["o"], i, o, EB)
                nc.vector.reciprocal(e_rs[:, b, 0:1], e_dev[:, b:b + 1]).then_inc(s["factor"], 1)

            def tile_bias(s, i, o):
                if skip(i, o, TILES):
                    return
                t, k, b = at(i, o, EB)
                dve.wait_ge(s["factor"], 2 * t + 1)
                nc.vector.scalar_tensor_tensor(e_rs[:, b, 1:2], e_mv[:, b, 0:1], -1.0, e_rs[:, b, 0:1],
                                               ALU.mult, ALU.mult).then_inc(s["factor"], 1)

            def row_variance(s, steps, i, o):
                if skip(i, o, TILES):
                    return
                t, k, b = at(i, o, EB)
                dve.wait_ge(s["fin"], steps * (t + 1) - 1)
                settle(dve)
                nc.vector.bn_aggr(e_mv[:, b, :], e_st[:, :]).then_inc(s["fin"], 1)

            def g_rows(i, o):
                have = not skip(i, o, TILES)
                if have:
                    t, k, b = at(i, o, EB)
                    dve.wait_ge(G0["deg"], t + 1)
                    dve.wait_ge(G0["dst_biased"], t + 1)
                    freed(dve, G0["o"], i, o, EB)
                    if not (isinstance(i, int) and o < 1):
                        dve.wait_ge(G0["fin"], FIN_STEPS[0] * t)
                    ch = Steps(dve, G0["fin"], t, FIN_STEPS[0])
                    ch.end(nc.vector.tensor_scalar(e_nrm[:, 0:1], e_sd[:, b:b + 1], 1.0, None, ALU.max))
                tile_scale(G0, i, o - 1)
                if have:
                    ch.start()
                    ch.end(nc.vector.reciprocal(e_nrm[:, 0:1], e_nrm[:, 0:1]))
                tile_bias(G0, i, o - 1)
                if have:
                    ch.start()
                    ch.end(nc.vector.scalar_tensor_tensor(e_z[:, b, :], bank[GTOT_BANK[b % 2]][:, 0:D], e_nrm[:, 0:1], e_dst[:, b, :],
                                                          ALU.mult, ALU.add))
                equal(G0, i, o + 2)
                if have:
                    ch.start()
                    ch.end(nc.vector.bn_stats(e_st[:, :], e_z[:, b, :]))

            def first_pass(i, o):
                group_scale(0, i, o + 2)
                group_variances(1, i, o - 2)
                group_bias(0, i, o + 2)
                group_moments(0, i, o + 3)
                group_scale(1, i, o - 2)
                group_variances(0, i, o + 3)
                group_bias(1, i, o - 2)
                low_parts(x1T_hi, x1T_lo, h_psum, d_x1T, i, o + 1)
                rows_low(G0, "M_psum", ((e_inT, bank[GT_BANK][:, :]),), i, o + 1)
                y_sum(i, o - 1)
                g_rows(i, o - 2)
                low_parts(hT_hi, hT_lo, y_psum, d_hT, i, o)
                row_variance(G0, FIN_STEPS[0], i, o - 2)
                group_moments(1, i, o - 1)
            run(dve, first_pass, GROUPS, 3, 3, TILES - GROUPS)

            dve.wait_ge(ends_in, 16 * 5)
            ch = Chain(dve, m_step, 0, 13)
            for r, lo in ((0, 0), (1, 2)):
                ch.add(nc.vector.tensor_tensor(m_same[:, r, :], m_dst[:, 1:P + 1], m_dst[:, lo:lo + P], ALU.is_equal))
                ch.add(nc.vector.tensor_scalar(m_same[:, r, :], m_same[:, r, :], 2 * BIG, -BIG, ALU.mult, ALU.add))
            first, last, prev_last, next_first = (m_edge[:, r, :] for r in range(4))
            for g, x, y in ((0, last, prev_last), (1, first, prev_last)):
                ch.add(nc.vector.tensor_tensor(m_gate[0:32, g, :], x[0:32], y[0:32], ALU.is_equal))
                ch.add(nc.vector.tensor_scalar(m_gate[0:32, g, :], m_gate[0:32, g, :], 2 * BIG, -BIG, ALU.mult, ALU.add))
            for g, x, y in ((0, first, next_first), (1, last, next_first)):
                ch.add(nc.vector.tensor_tensor(m_gate[32:64, g, :], x[32:64], y[32:64], ALU.is_equal))
                ch.add(nc.vector.tensor_scalar(m_gate[32:64, g, :], m_gate[32:64, g, :], 2 * BIG, -BIG, ALU.mult, ALU.add))
            ch.add(nc.vector.memset(m_end[:, :], 0.0))

            for l in range(2):
                s, c, m = A[l], CB[l], SM[l]

                def attend(i, o):
                    rows_low(s, "v_psum", transposed(o + 1), i, o + 1)
                    if skip(i, o, TILES):
                        return
                    t, k, b = at(i, o, EB)
                    v = bank[(2, 7)[b % 2]]
                    dve.wait_ge(s["e_out"], t + 1)
                    dve.wait_ge(s["qs_out"], t + 1)
                    if not (isinstance(i, int) and o < 1):
                        dve.wait_ge(s["score"], SCORE_STEPS * t)
                    ch = Steps(dve, s["score"], t, SCORE_STEPS)
                    ch.start()
                    ch.end(nc.vector.tensor_tensor(e_prod[:, :], bank[3 + b % 2][:, 0:D], e_edge[:, b, :], ALU.add))
                    settle(dve)
                    nc.vector.tensor_tensor(vals[:, bass.ds(t * D, D)], v[:, 0:D], e_edge[:, b, :], ALU.add).then_inc(s["v_out"], 1)
                    ch.start()
                    ch.end(nc.vector.tensor_tensor(e_prod[:, :], e_prod[:, :], e_qs[:, b, 0:D], ALU.mult))
                    if l:
                        arrived(dve, s, "res_in", k, b)
                        nc.vector.tensor_tensor(e_qs[:, b, D:2 * D], e_qs[:, b, D:2 * D], e_res[:, b, :], ALU.add).then_inc(s["res_added"], 1)
                    ch.start()
                    settle(dve)
                    ch.end(nc.vector.tensor_reduce(alpha[:, bass.ds(t * H, H)], e_prod[:, :].rearrange("p (h c) -> p h c", h=H), AX.X, ALU.add))
                run(dve, attend, TILES, 0, 1)

                dve.wait_ge(s["score"], SCORE_STEPS * TILES)
                nc.vector.memset(alpha[0:1, :], -BIG).then_inc(m["masked"], 1)
                ch = Chain(dve, m["step"], 0, SM_STEPS)
                dve.wait_ge(m["aT"], 1)
                ch.add(nc.vector.tensor_copy(m_a[:, :], bank[7][0:TILES, :]))

                def scans(carried):
                    for h in range(H):
                        f = m_f[:, h * P:(h + 1) * P]
                        r = m_r[:, h * P:(h + 1) * P]
                        x = m_a[:, h * P:(h + 1) * P]
                        nc.vector.tensor_tensor_scan(f, m_same[:, 0, :], x, m_cin[:, h:h + 1] if carried else -BIG, ALU.min, ALU.max)
                        last = nc.vector.tensor_tensor_scan(r[:, ::-1], m_same[:, 1, ::-1], x[:, ::-1],
                                                            m_cin[:, 32 + h:33 + h] if carried else -BIG, ALU.min, ALU.max)
                    ch.add(last)
                scans(False)
                ch.add(nc.vector.tensor_copy(m_end[:, 0:H], m_f.rearrange("t (h s) -> t h s", h=H)[:, :, P - 1]))
                ch.add(nc.vector.tensor_copy(m_end[:, 32:32 + H], m_r.rearrange("t (h s) -> t h s", h=H)[:, :, 0]))
                dve.wait_ge(m["ends"], 1)
                ch.add(nc.vector.tensor_copy(m_rows[:, :], bank[0][0:64, 0:TILES]))
                fw, bw = slice(0, 32), slice(32, 64)
                ch.add(nc.vector.tensor_tensor_scan(m_scan[fw, :], m_gate[fw, 0, :], m_rows[fw, :], -BIG, ALU.min, ALU.max))
                ch.add(nc.vector.tensor_tensor_scan(m_scan[bw, ::-1], m_gate[bw, 0, ::-1], m_rows[bw, ::-1], -BIG, ALU.min, ALU.max))
                ch.add(nc.vector.memset(m_in[:, :], -BIG))
                ch.add(nc.vector.tensor_tensor(m_in[fw, 1:TILES], m_scan[fw, 0:TILES - 1], m_gate[fw, 1, 1:TILES], ALU.min))
                ch.add(nc.vector.tensor_tensor(m_in[bw, 0:TILES - 1], m_scan[bw, 1:TILES], m_gate[bw, 1, 0:TILES - 1], ALU.min))
                dve.wait_ge(m["cin"], 1)
                ch.add(nc.vector.tensor_copy(m_cin[:, :], bank[1][0:TILES, 0:64]))
                scans(True)
                ch.add(nc.vector.tensor_tensor(m_f[:, :], m_f[:, :], m_r[:, :], ALU.max))
                dve.wait_ge(m["max_psum"], 1)
                nc.vector.tensor_tensor(ex.rearrange("p (t h) -> p h t", h=H), alpha.rearrange("p (t h) -> p h t", h=H),
                                        bank[7][:, 0:H * TILES].rearrange("p (h t) -> p h t", h=H), ALU.subtract).then_inc(m["max"], 1)

                def combine(i, o):
                    have = not skip(i, o - 1, TILES)
                    if have:
                        t, k, b = at(i, o - 1, EB)
                        tot = bank[b]
                        dve.wait_ge(c["tot"], t + 1)
                        if not (isinstance(i, int) and o == TILES):
                            dve.wait_ge(c["carry"], t + 2)
                        arrived(dve, c, "self_in", k, b)
                        freed(dve, c["o"], i, o - 1, EB)
                        if not (isinstance(i, int) and o <= 1):
                            dve.wait_ge(c["fin"], FIN_STEPS[1 + l] * t)
                        ch = Steps(dve, c["fin"], t, FIN_STEPS[1 + l])
                        ch.start()
                        ch.end(nc.vector.tensor_scalar(e_nrm[:, 0:H], tot[:, D:CW], SOFTMAX_EPS, None, ALU.add))
                    if l:
                        tile_scale(c, i, o - 3)
                    if have:
                        ch.start()
                        ch.end(nc.vector.reciprocal(e_nrm[:, 0:H], e_nrm[:, 0:H]))
                    if l:
                        tile_bias(c, i, o - 3)
                    if not l:
                        equal(c, i, o + 2)
                    if have:
                        ch.start()
                        for h in range(H):
                            col = slice(h * C, (h + 1) * C)
                            last = nc.vector.scalar_tensor_tensor(e_z[:, b, col], tot[:, col], e_nrm[:, h:h + 1],
                                                                  e_res[:, b, col], ALU.mult, ALU.add)
                        ch.end(last)
                        if l:
                            ch.start()
                            ch.end(nc.vector.bn_stats(e_st[:, :], e_z[:, b, :]))
                    if l:
                        equal(c, i, o + 2)
                        row_variance(c, FIN_STEPS[2], i, o - 1)
                run(dve, combine, TILES, 1 + 2 * l, 2)

        @block.tensor
        def _(pe):
            pe.wait_ge(ident_done, 2)
            pe.wait_ge(prep_done, 5)
            pe.wait_ge(weights_lo, 3)
            pe.wait_ge(bias_moved, 16 * 4)

            def transpose_group(src, done, i, o, ready, read, before, times):
                if skip(i, o, GROUPS):
                    return
                g, k, b = at(i, o, DB)
                pe.wait_ge(ready, (g + 1) * times)
                n = g - before
                if not (isinstance(i, int) and not 0 <= n < GROUPS):
                    pe.wait_ge(read, 2 * (n + 1))
                for kk in range(2):
                    for j in range(J):
                        last = nc.tensor.transpose(bank[T_BANK[kk]][:, j * P:(j + 1) * P],
                                                   src[:, b, j * D + kk * P:j * D + (kk + 1) * P], ident[:, :])
                last.then_inc(done, 1)

            def product(srcT, layer, done, i, o, parts, read, before, times):
                if skip(i, o, GROUPS):
                    return
                g, k, b = at(i, o, DB)
                pe.wait_ge(parts, 2 * (g + 1))
                n = g - before
                for m in range(2):
                    if not (isinstance(i, int) and not 0 <= n < GROUPS):
                        pe.wait_ge(read, n * times + m + 1)
                    for jj in range(2):
                        j = 2 * m + jj
                        dst = bank[W_BANK[m]][:, jj * D:(jj + 1) * D]
                        nc.tensor.matmul(dst, ones_bf[:, :], bias_mm[:, 2 * layer, D:2 * D], start=True, stop=False)
                        for d, w in PASSES:
                            for kk in range(2):
                                last = nc.tensor.matmul(dst, srcT[:, b % 2, d, kk * GROUP + j * P:kk * GROUP + (j + 1) * P],
                                                        w_qs[layer][:, w, kk, D:2 * D], start=False,
                                                        stop=(d, w, kk) == (HI, HI, 1))
                    last.then_inc(done, 1)

            def sums(s, rhs, width, tot, free, i, o):
                if skip(i, o, TILES):
                    return
                t, k, b = at(i, o, EB)
                pe.wait_ge(s["eq"], t + 1)
                pe.wait_ge(s["carry"], t + 1)
                freed(pe, s["fin"], i, o, free[0], free[1])
                nc.tensor.matmul(tot[:, 0:width], e_eq[:, b, :], rhs[:, b, 0:width], start=True, stop=True).then_inc(s["tot"], 1)

            def cols(t, b, k):
                return t[:, b, k * P:(k + 1) * P]

            def part_cols(b, part, k):
                return e_inT[:, b % 2, part, k * P:(k + 1) * P]

            def g_transposes(i, o):
                if skip(i, o, TILES):
                    return
                t, k, b = at(i, o, EB)
                arrived(pe, G0, "src_in", k, b)
                arrived(pe, G0, "attr_in", k, b)
                freed(pe, G0["T_lo"], i, o, 1)
                for kk in range(4):
                    last = nc.tensor.transpose(cols_of(bank[GT_BANK], kk), cols((e_src, e_attr)[kk // 2], b, kk % 2), ident[:, :])
                last.then_inc(G0["T_psum"], 1)

            def cols_of(t, k):
                return t[:, k * P:(k + 1) * P]

            def messages(i, o):
                if skip(i, o, TILES):
                    return
                t, k, b = at(i, o, EB)
                pe.wait_ge(G0["T_lo"], t + 1)
                freed(pe, G0["rhs_in"], i, o, 1)
                for d, w in PASSES:
                    for kk in range(4):
                        last = nc.tensor.matmul(bank[GM_BANK][:, 0:D], part_cols(b, d, kk), w0[:, w, kk, :],
                                                start=(d, w, kk) == (LO, HI, 0), stop=(d, w, kk) == (HI, HI, 3))
                last.then_inc(G0["M_psum"], 1)

            def first_pass(i, o):
                product(d_x1T, 0, h_psum, i, o, x1T_lo, y_step, 2, Y_STEPS)
                transpose_group(d_x1, x1T_psum, i, o + 1, x1_done, hT_lo, 2, 1)
                g_transposes(i, o + 1)
                product(d_hT, 1, y_psum, i, o - 1, hT_lo, h_done, -1, 2)
                transpose_group(d_h, hT_psum, i, o, h_done, x1T_lo, -1, 2)
                messages(i, o)
                sums(G0, e_rhs, D + 1, bank[GTOT_BANK[(o - 1) % 2]], (2, FIN_STEPS[0]), i, o - 1)
            run(pe, first_pass, GROUPS, 1, 1, TILES - GROUPS)

            pe.wait_ge(weights_lo, len(raw_weights))
            for l in range(2):
                s, c, m = A[l], CB[l], SM[l]

                def transposes(i, o):
                    if skip(i, o, TILES):
                        return
                    t, k, b = at(i, o, EB)
                    for n in ("src_in", "attr_in", "dst_in"):
                        arrived(pe, s, n, k, b)
                    freed(pe, s["T_lo"], i, o, 2)
                    if not (isinstance(i, int) and o < 2):
                        pe.wait_ge(s["score"], SCORE_STEPS * (t - 2) + 1)
                    for kk in range(4):
                        nc.tensor.transpose(cols_of(bank[o % 2], kk), cols((e_src, e_dst)[kk // 2], b, kk % 2), ident[:, :])
                    nc.tensor.transpose(bank[3 + o % 2][:, D:D + P], e_attr[:, b, 0:P], ident[:, :]).then_inc(s["T_psum"], 1)

                def attend(i, o):
                    if skip(i, o, TILES):
                        transposes(i, o + 1)
                        return
                    t, k, b = at(i, o, EB)
                    q = o % 2
                    pe.wait_ge(s["T_lo"], t + 1)
                    freed(pe, s["qs_out"], i, o, 2)

                    def project(out_, bias, w, col, first):
                        width = out_.shape[-1]
                        nc.tensor.matmul(out_, ones_bf[:, :], bias, start=True, stop=False)
                        for d, p in PASSES:
                            for kk in range(2):
                                last = nc.tensor.matmul(out_, part_cols(b, d, first + kk), w[:, p, kk, col:col + width],
                                                        start=False, stop=(d, p, kk) == (HI, HI, 1))
                        return last

                    project(bank[5 + q][:, :], bias_mm[:, 2 * l, :], w_qs[l], 0, 2).then_inc(s["qs_psum"], 1)
                    transposes(i, o + 1)
                    project(bank[3 + q][:, 0:D], bias_mm[:, 2 * l + 1, 0:D], w_kv[l], 0, 0)
                    freed(pe, s["v_out"], i, o, 2)
                    v = bank[(2, 7)[q]]
                    for d, p in PASSES:
                        nc.tensor.matmul(v[:, D:2 * D], e_atT[:, q, d, :], w_e[l][:, p, 0, :], start=(d, p) == (LO, HI),
                                         stop=(d, p) == (HI, HI))
                    project(v[:, 0:D], bias_mm[:, 2 * l + 1, D:2 * D], w_kv[l], D, 0).then_inc(s["v_psum"], 1)
                run(pe, attend, TILES, 0, 1)

                pe.wait_ge(m["masked"], 1)
                pe.wait_ge(s["v_out"], TILES)
                for h in range(H):
                    last = nc.tensor.transpose(bank[7][0:TILES, h * P:(h + 1) * P], alpha.rearrange("p (t h) -> p h t", h=H)[:, h, :], ident[:, :])
                last.then_inc(m["aT"], 1)
                pe.wait_ge(m["step"], 4)
                nc.tensor.transpose(bank[0][:, 0:TILES], m_end[:, :], ident[0:TILES, 0:TILES]).then_inc(m["ends"], 1)
                pe.wait_ge(m["step"], 10)
                nc.tensor.matmul(bank[1][0:TILES, 0:64], m_in[:, :], ident[0:64, 0:64], start=True, stop=True).then_inc(m["cin"], 1)
                pe.wait_ge(m["step"], SM_STEPS)
                for h in range(H):
                    last = nc.tensor.transpose(bank[7][:, h * TILES:(h + 1) * TILES], m_f[:, h * P:(h + 1) * P], ident[0:TILES, 0:TILES])
                last.then_inc(m["max_psum"], 1)
                run(pe, lambda i, o: sums(c, e_rhs, CW, bank[o % EB], (EB, FIN_STEPS[1 + l]), i, o), TILES, 0, 0)


SPLIT_STEPS = 1 + 1 + 5
SM_STEPS = 13

def layout(inputs):
    pad = N

    def rows(v, fill):
        full = np.full((TILES * EPT,) + v.shape[1:], fill, v.dtype)
        full[:E] = v
        return full.reshape((TILES, EPT) + v.shape[1:])

    def attr(v):
        slots = np.zeros((TILES, P, v.shape[1]), v.dtype)
        slots[:, 1:] = rows(v, 0)
        return slots.reshape(TILES * P, v.shape[1])

    dst = rows(np.asarray(inputs["dst"]), pad)
    src = rows(np.asarray(inputs["src"]), 0)
    none = np.full((1,), -1, dst.dtype)
    after = np.concatenate([dst.reshape(-1)[1:], none]).reshape(TILES, EPT)
    first, last = dst[:, 0], dst[:, -1]
    next_first = np.concatenate([first[1:], none])
    prev_last = np.concatenate([none, last[:-1]])
    slots = np.concatenate([first[:, None], dst], 1)
    return {
        "src_slots": np.concatenate([src[:, :1], src], 1).T,
        "dst_slots": slots.T,
        "dst_next": np.concatenate([first[:, None], after], 1).T,
        "dst_rows": np.concatenate([next_first[:, None], dst], 1),
        "dst_tiles": np.concatenate([first[:, None], slots, last[:, None]], 1),
        "tile_ends": np.stack([first, last, prev_last, next_first]),
        "attr_128": attr(np.asarray(inputs["edge_attr_128"])),
        "attr_256": attr(np.asarray(inputs["edge_attr_256"])),
    }


def kernel(**inputs):
    import concourse.bacc as bacc
    from concourse import mybir as mb
    from concourse.bass_utils import run_bass_kernel_spmd

    arrays = {n: np.asarray(v) for n, v in inputs.items() if n not in ("src", "dst", "edge_attr_128", "edge_attr_256")}
    arrays.update(layout(inputs))
    arrays = {f"in_{n}": np.ascontiguousarray(v) for n, v in arrays.items()}
    nc = bacc.Bacc("TRN2", target_bir_lowering=False, num_devices=1)
    args = {n[3:]: nc.dram_tensor(n, v.shape, mb.dt.from_np(v.dtype), kind="ExternalInput").ap() for n, v in arrays.items()}
    out = nc.dram_tensor("out", (N, D), mb.dt.float32, kind="ExternalOutput").ap()
    build(nc, args, out)
    return run_bass_kernel_spmd(nc, [arrays], core_ids=[0]).results[0]["out"]
```
